# Optimizing a Trainium2 kernel written in Bass

```python
import numpy as np
import jax
import jax.numpy as jnp

def _softmax(x, axis=-1):
    return jax.nn.softmax(x, axis=axis)

def _gelu(x):
    return jax.nn.gelu(x, approximate=True)

def _silu(x):
    return jax.nn.silu(x)

def _sigmoid(x):
    return jax.nn.sigmoid(x)

def _layernorm(x, axis=-1, eps=1e-05):
    m = jnp.mean(x, axis=axis, keepdims=True)
    v = jnp.var(x, axis=axis, keepdims=True)
    return (x - m) / jnp.sqrt(v + eps)

def _scatter_add(tgt, idx, src, axis=0):
    return tgt.at[idx].add(src)

def _segment_sum(src, seg, n):
    return jax.ops.segment_sum(src, seg, n)
kernel_name = 'mk_gnn_resnorm_d1_gnn_r16_65e711'

def setup_inputs(seed: int=0):
    np.random.seed(seed)
    _w = jnp.asarray

    def _rec_inputs():
        import jax
        import jax.numpy as jnp
        _gk = jax.random.key(seed)
        x = -0.000202 + 1 * jax.random.normal(jax.random.fold_in(_gk, 1), (3125, 128), jnp.float32)
        src = jax.random.randint(jax.random.fold_in(_gk, 2), (100000,), 0, 3125, jnp.int32)
        dst = jax.random.randint(jax.random.fold_in(_gk, 3), (100000,), 0, 3125, jnp.int32)
        _o = jnp.argsort(dst, stable=True)
        src = src[_o]
        dst = dst[_o]
        return (x, src, dst)
    x, src, dst = _rec_inputs()

    def _L0_gnn_setup():
        import jax, jax.numpy as jnp
        import numpy as np
        N_NODES = 3125
        N_EDGES = 50000
        DIM = 128
        HEADS = 2
        DEPTH = 2
        MLP = 512
        NEG_SLOPE = 0.2
        EPS = 1e-05

        def _layer_norm(x, g, b):
            m = jnp.mean(x, axis=-1, keepdims=True)
            v = jnp.var(x, axis=-1, keepdims=True)
            return (x - m) * jax.lax.rsqrt(v + EPS) * g + b

        def _gatv2(x, src, dst, Wl, bl, Wr, br, att, gat_b):
            n = x.shape[0]
            xl = (x @ Wl + bl).reshape(n, HEADS, DIM)
            xr = (x @ Wr + br).reshape(n, HEADS, DIM)
            e = jax.nn.leaky_relu(xl[src] + xr[dst], NEG_SLOPE)
            score = jnp.einsum('ehd,hd->eh', e, att)
            smax = jax.ops.segment_max(score, dst, num_segments=n)
            ex = jnp.exp(score - smax[dst])
            denom = jax.ops.segment_sum(ex, dst, num_segments=n)
            alpha = ex / (denom[dst] + 1e-16)
            msg = xl[src] * alpha[..., None]
            out = jax.ops.segment_sum(msg, dst, num_segments=n)
            return out.reshape(n, HEADS * DIM) + gat_b
        key = jax.random.key(seed)
        ks = jax.random.split(key, 10)
        s = 0.05
        p = lambda k, shape: jax.random.normal(k, shape, jnp.float32) * s
        x = jax.random.normal(ks[0], (N_NODES, DIM), jnp.float32)
        edge_index = jax.random.randint(ks[1], (2, N_EDGES), 0, N_NODES, dtype=jnp.int64)
        D, H = (DEPTH, HEADS)
        return {'x': x, 'edge_index': edge_index, 'ln1_g': jnp.ones((D, DIM), jnp.float32), 'ln1_b': jnp.zeros((D, DIM), jnp.float32), 'Wl': p(ks[2], (D, DIM, H * DIM)), 'bl': jnp.zeros((D, H * DIM), jnp.float32), 'Wr': p(ks[3], (D, DIM, H * DIM)), 'br': jnp.zeros((D, H * DIM), jnp.float32), 'att': p(ks[4], (D, H, DIM)), 'gat_b': jnp.zeros((D, H * DIM), jnp.float32), 'proj_W': p(ks[5], (D, H * DIM, DIM)), 'proj_b': jnp.zeros((D, DIM), jnp.float32), 'ln2_g': jnp.ones((D, DIM), jnp.float32), 'ln2_b': jnp.zeros((D, DIM), jnp.float32), 'W1': p(ks[6], (D, DIM, MLP)), 'b1': jnp.zeros((D, MLP), jnp.float32), 'W2': p(ks[7], (D, MLP, DIM)), 'b2': jnp.zeros((D, DIM), jnp.float32)}
    _L0_gnn_all = _L0_gnn_setup()
    _L0_gnn_in = {k: v for k, v in _L0_gnn_all.items() if k in ('ln1_g', 'ln1_b', 'Wl', 'bl', 'Wr', 'br', 'att', 'gat_b', 'proj_W', 'proj_b', 'ln2_g', 'ln2_b', 'W1', 'b1', 'W2', 'b2')}
    del _L0_gnn_all
    return {'x': x, 'src': src, 'dst': dst, 'L0_gnn_ln1_g': _L0_gnn_in['ln1_g'], 'L0_gnn_ln1_b': _L0_gnn_in['ln1_b'], 'L0_gnn_Wl': _L0_gnn_in['Wl'], 'L0_gnn_bl': _L0_gnn_in['bl'], 'L0_gnn_Wr': _L0_gnn_in['Wr'], 'L0_gnn_br': _L0_gnn_in['br'], 'L0_gnn_att': _L0_gnn_in['att'], 'L0_gnn_gat_b': _L0_gnn_in['gat_b'], 'L0_gnn_proj_W': _L0_gnn_in['proj_W'], 'L0_gnn_proj_b': _L0_gnn_in['proj_b'], 'L0_gnn_ln2_g': _L0_gnn_in['ln2_g'], 'L0_gnn_ln2_b': _L0_gnn_in['ln2_b'], 'L0_gnn_W1': _L0_gnn_in['W1'], 'L0_gnn_b1': _L0_gnn_in['b1'], 'L0_gnn_W2': _L0_gnn_in['W2'], 'L0_gnn_b2': _L0_gnn_in['b2']}

def reference(x, src, dst, L0_gnn_ln1_g, L0_gnn_ln1_b, L0_gnn_Wl, L0_gnn_bl, L0_gnn_Wr, L0_gnn_br, L0_gnn_att, L0_gnn_gat_b, L0_gnn_proj_W, L0_gnn_proj_b, L0_gnn_ln2_g, L0_gnn_ln2_b, L0_gnn_W1, L0_gnn_b1, L0_gnn_W2, L0_gnn_b2):
    import jax
    import jax.numpy as jnp

    def _L0_gnn_ref(x, edge_index, ln1_g, ln1_b, Wl, bl, Wr, br, att, gat_b, proj_W, proj_b, ln2_g, ln2_b, W1, b1, W2, b2):
        import jax, jax.numpy as jnp
        import numpy as np
        N_NODES = 3125
        N_EDGES = 50000
        DIM = 128
        HEADS = 2
        DEPTH = 2
        MLP = 512
        NEG_SLOPE = 0.2
        EPS = 1e-05

        def _layer_norm(x, g, b):
            m = jnp.mean(x, axis=-1, keepdims=True)
            v = jnp.var(x, axis=-1, keepdims=True)
            return (x - m) * jax.lax.rsqrt(v + EPS) * g + b

        def _gatv2(x, src, dst, Wl, bl, Wr, br, att, gat_b):
            n = x.shape[0]
            xl = (x @ Wl + bl).reshape(n, HEADS, DIM)
            xr = (x @ Wr + br).reshape(n, HEADS, DIM)
            e = jax.nn.leaky_relu(xl[src] + xr[dst], NEG_SLOPE)
            score = jnp.einsum('ehd,hd->eh', e, att)
            smax = jax.ops.segment_max(score, dst, num_segments=n)
            ex = jnp.exp(score - smax[dst])
            denom = jax.ops.segment_sum(ex, dst, num_segments=n)
            alpha = ex / (denom[dst] + 1e-16)
            msg = xl[src] * alpha[..., None]
            out = jax.ops.segment_sum(msg, dst, num_segments=n)
            return out.reshape(n, HEADS * DIM) + gat_b
        src, dst = (edge_index[0], edge_index[1])
        for i in range(DEPTH):
            h = _layer_norm(x, ln1_g[i], ln1_b[i])
            g = _gatv2(h, src, dst, Wl[i], bl[i], Wr[i], br[i], att[i], gat_b[i])
            x = x + (g @ proj_W[i] + proj_b[i])
            h = _layer_norm(x, ln2_g[i], ln2_b[i])
            x = x + (jax.nn.gelu(h @ W1[i] + b1[i]) @ W2[i] + b2[i])
        return x
    edge_index = jnp.stack([src, dst])
    x = _layernorm(x + _L0_gnn_ref(x, edge_index, L0_gnn_ln1_g, L0_gnn_ln1_b, L0_gnn_Wl, L0_gnn_bl, L0_gnn_Wr, L0_gnn_br, L0_gnn_att, L0_gnn_gat_b, L0_gnn_proj_W, L0_gnn_proj_b, L0_gnn_ln2_g, L0_gnn_ln2_b, L0_gnn_W1, L0_gnn_b1, L0_gnn_W2, L0_gnn_b2), axis=-1)
    return x

_drawn_inputs = setup_inputs


def setup_inputs(seed=0):
    import zlib

    import numpy as np

    out = dict(_drawn_inputs(seed))
    spreads = {'L0_gnn_ln1_g': (1.0, 0.6),
     'L0_gnn_ln1_b': (0.0, 0.1),
     'L0_gnn_bl': (0.0, 0.1),
     'L0_gnn_br': (0.0, 2.0),
     'L0_gnn_gat_b': (0.0, 0.1),
     'L0_gnn_proj_b': (0.0, 0.1),
     'L0_gnn_ln2_g': (1.0, 0.2),
     'L0_gnn_ln2_b': (0.0, 0.1),
     'L0_gnn_b1': (0.0, 0.1),
     'L0_gnn_b2': (0.0, 0.1)}
    factors = {'L0_gnn_Wr': 8.0, 'L0_gnn_att': 3.514}
    for name, (base, spread) in spreads.items():
        noise = np.random.default_rng([zlib.crc32(name.encode()), seed]).standard_normal(out[name].shape)
        drawn = base * np.exp(spread * noise) if base else spread * noise
        out[name] = jnp.asarray(drawn.astype(out[name].dtype))
    for name, factor in factors.items():
        out[name] = (out[name] * factor).astype(out[name].dtype)
    return out
```

```python
from contextlib import ExitStack
from functools import partial

import concourse.bass as bass
from concourse import mybir

F32 = mybir.dt.float32
BF16 = mybir.dt.bfloat16
I32 = mybir.dt.int32
I16 = mybir.dt.int16
ALU = mybir.AluOpType
ACT = mybir.ActivationFunctionType
AX = mybir.AxisListType.X

P = 128
N, D, H, L, MLP, E = 3125, 128, 2, 2, 512, 100000
HD = H * D
EPS = 1e-5
SLOPE = 0.2

K = 2
UE = K * P
NU = -(-E // UE)
W = 32
HW = H * W
NB = -(-N // W)
NT = -(-N // P)
NBP = NT * P // W
RING = 6
LAG = 4
GROUPS = -(-(NU + NB - 1) // RING)
NS = GROUPS * RING
TABW = 512
TJ = -(-E // (P * P))
EFULL = (TJ - 1) * P * P
ETILES = (E - EFULL) // P
EREST = E - EFULL - ETILES * P
RC = D + 2
XC = HD + H
MASK = 1e30
FLOOR = -1e20
UT = 5
assert NT % UT == 0 and NS <= TABW


def gnn(nc, x, src, dst, ln1_g, ln1_b, Wl, bl, Wr, br, att, gat_b, proj_W, proj_b, ln2_g, ln2_b, W1, b1,
        W2, b2, out):
    table = nc.dram_tensor("table", (NT * P, H * RC), F32, kind="Internal").ap()
    xr_split = nc.dram_tensor("xr_split", (3, NT * P, XC), BF16, kind="Internal").ap()
    dst16 = nc.dram_tensor("dst16", (TJ * P * P,), I16, kind="Internal").ap()
    tabs_d = nc.dram_tensor("tabs_d", (2, TABW), I32, kind="Internal").ap()

    with ExitStack() as ctx:
        def sb(name, shape, dt):
            return ctx.enter_context(nc.sbuf_tensor(name, shape, dt))

        ident = sb("ident", [P, P], F32)
        ones = sb("ones", [P, P], F32)
        node_row = sb("node_row", [P, NB * W], F32)
        node_col = sb("node_col", [3 * W, NB], F32)
        src_t = sb("src_t", [P, TJ * P], I32)
        dst_t = sb("dst_t", [P, TJ * P], F32)
        tab_u = sb("tab_u", [1, TABW], I32)
        tab_b = sb("tab_b", [1, TABW], I32)
        tab_b0 = sb("tab_b0", [1, TABW], I32)
        flag_row = sb("flag_row", [1, TABW], I32)
        n_pass_t = sb("n_pass_t", [1, 1], I32)
        eps_t = sb("eps_t", [P, 1], F32)
        xs = sb("xs", [P, NT, P], F32)
        xc = sb("xc", [P, NT, P], F32)
        mean = sb("mean", [P, NT], F32)
        rstd = sb("rstd", [P, NT], F32)
        acc = sb("acc", [HW, NBP, D + 1], F32)
        run_max = sb("run_max", [HW, NBP], F32)
        xr3 = sb("xr3", [3 * W, NB, XC], BF16)

        psum_z = [ctx.enter_context(nc.psum_tensor(f"psum{i}", [P, 512], F32)) for i in range(8)]

        sems = []

        def end_phase():
            nc.gpsimd.dma_reset(range(sems[0].num, sems[-1].num + 1))
            nc.gpsimd.sem_clear(range(sems[0].num, sems[-1].num + 1))
            nc.all_engine_barrier()
            sems.clear()

        names = [0]

        def scratch(build, *args):
            names[0] += 1
            with ExitStack() as inner:
                def sbi(name, shape, dt):
                    return inner.enter_context(nc.sbuf_tensor(f"{name}_{names[0]}", shape, dt))
                with ExitStack() as si:
                    def semi(name):
                        sems.append(si.enter_context(nc.semaphore(f"{name}_{names[0]}")))
                        return sems[-1]
                    build(nc, sbi, semi, psum_z, *args)
                    end_phase()

        scratch(setup, dict(x=x, src=src, dst=dst, dst16=dst16, tabs_d=tabs_d, ident=ident, ones=ones,
                                        node_row=node_row, node_col=node_col, src_t=src_t, dst_t=dst_t, tab_u=tab_u,
                                        tab_b0=tab_b0, flag_row=flag_row, n_pass_t=n_pass_t, eps_t=eps_t, xs=xs))
        n_pass = nc.values_load(n_pass_t[0:1, 0:1], min_val=1, max_val=NB)

        wlr = sb("wlr", [P, 2 * HD], F32)
        blr = sb("blr", [P, 2 * HD], F32)
        att_row = sb("att_row", [P, HD], F32)
        gcol = sb("gcol", [P, 4], F32)
        gat_col = sb("gat_col", [P, H], F32)
        b1_col = sb("b1_col", [P, 4], F32)
        pw = sb("pw", [P, H, P], F32)
        w1 = sb("w1", [P, MLP], F32)
        w2 = sb("w2", [P, MLP // P, P], F32)
        pb_row = sb("pb_row", [P, P], F32)
        b2_row = sb("b2_row", [P, P], F32)
        wts = dict(wlr=wlr, blr=blr, att_row=att_row, gcol=gcol, gat_col=gat_col, b1_col=b1_col, pw=pw, w1=w1,
                   w2=w2, pb_row=pb_row, b2_row=b2_row, Wl=Wl, Wr=Wr, bl=bl, br=br, att=att, gat_b=gat_b,
                   proj_W=proj_W, proj_b=proj_b, ln1_g=ln1_g, ln1_b=ln1_b, ln2_g=ln2_g, ln2_b=ln2_b, W1=W1, b1=b1,
                   W2=W2, b2=b2)
        st = dict(ident=ident, ones=ones, xs=xs, xc=xc, mean=mean, rstd=rstd, eps_t=eps_t, table=table,
                  xr_split=xr_split, xr3=xr3, acc=acc, run_max=run_max, node_row=node_row, node_col=node_col,
                  src_t=src_t, dst_t=dst_t, att_row=att_row, tab_u=tab_u, tab_b=tab_b, tab_b0=tab_b0, flag_row=flag_row, dst16=dst16)

        with nc.Fori(0, L) as layer:
            scratch(project_nodes, wts, st, layer)
            with nc.Fori(0, n_pass) as _:
                scratch(edge_pass, st)
            scratch(update_nodes, wts, st)
        scratch(finish, st, x, out)


def setup(nc, sb, sem, ps, g):
    sems_in = sem("lists_in")
    pads = sem("pads")
    consts = sem("consts")
    id_zero = sem("id_zero")
    cast = sem("cast")
    turned = sem("turned")
    copied = sem("copied")
    dst16_out = sem("dst16_out")
    step_ready = sem("step_ready")
    chain = sem("chain")
    tabs_out = sem("tabs_out")
    tabs_in = sem("tabs_in")
    sq = sem("sq")

    with ExitStack() as ctx:
        def tmp(name, shape, dt):
            return ctx.enter_context(nc.sbuf_tensor(name, shape, dt))
        dst_d = tmp("dst_d", [P, TJ, P], I32)
        nxt_d = tmp("nxt_d", [P, TJ, P], I32)
        src_d = tmp("src_d", [P, TJ, P], I32)
        dst_f = tmp("dst_f", [P, TJ, P], F32)
        nxt_f = tmp("nxt_f", [P, TJ, P], F32)
        src_f = tmp("src_f", [P, TJ, P], F32)
        dst_h = tmp("dst_h", [P, TJ, P], I16)
        uns = tmp("uns", [P, 1], F32)
        last_i = tmp("last_i", [1, NU], I32)
        last_b = tmp("last_b", [1, NU], I32)
        key = tmp("key", [1, NU], F32)
        unit_no = tmp("unit_no", [1, NU], F32)
        step_no = tmp("step_no", [P, 4], F32)
        junk = tmp("junk", [P, NU], F32)
        cnt = tmp("cnt", [P, 4], F32)
        flag = tmp("flag", [P, 1], F32)
        keep = tmp("keep", [P, 1], F32)
        lin = tmp("lin", [P, 4], F32)
        stair_b = tmp("stair_b", [P, 4], F32)
        tmp4 = tmp("tmp4", [P, 4], F32)
        tu = tmp("tu", [P, 4], F32)
        tabs = tmp("tabs", [P, 2, 4], I32)
        zero_row = tmp("zero_row", [1, TABW], F32)
        xs, src_t, dst_t = g["xs"], g["src_t"], g["dst_t"]
        NFULL = N // P

        with nc.Block() as block:
            @block.sync
            def _(sp):
                sp.wait_ge(pads, 4)
                for t, a, o in ((dst_d, g["dst"], 0), (nxt_d, g["dst"], 1), (src_d, g["src"], 0)):
                    sp.dma_start(t[:, 0:TJ - 1, :], a[o:EFULL + o].rearrange("(j c p) -> c j p", c=P, p=P)
                                 ).then_inc(sems_in, 16)
                    m = EFULL + ETILES * P
                    sp.dma_start(t[0:ETILES, TJ - 1, :], a[EFULL + o:m + o].rearrange("(c p) -> c p", p=P)
                                 ).then_inc(sems_in, 16)
                    sp.dma_start(t[ETILES:ETILES + 1, TJ - 1, 0:EREST - o],
                                 a[m + o:E].rearrange("(c p) -> c p", c=1)).then_inc(sems_in, 16)
                sp.dma_start(last_i[0:1, 0:NU - 1],
                             g["dst"][0:(NU - 1) * UE].rearrange("(a u q) -> a u q", q=UE, a=1)[:, :, UE - 1],
                             allow_slow_non_contiguous=True).then_inc(sems_in, 16)
                sp.dma_start(last_i[0:1, NU - 1:NU], g["dst"][E - 1:E].rearrange("(a u) -> a u", a=1)
                             ).then_inc(sems_in, 16)
                sp.dma_start(xs[:, 0:NFULL, :], g["x"][0:NFULL * P, :].rearrange("(t p) d -> p t d", p=P)
                             ).then_inc(sems_in, 16)
                sp.dma_start(xs[0:N - NFULL * P, NFULL, :], g["x"][NFULL * P:N, :]).then_inc(sems_in, 16)
                sp.wait_ge(cast, 1)
                sp.dma_start(g["dst16"].rearrange("(j c p) -> c j p", c=P, p=P), dst_h[:, :, :]
                             ).then_inc(dst16_out, 16)
                sp.wait_ge(step_ready, 1)
                for r in range(2):
                    sp.dma_start(g["tabs_d"][r, :].rearrange("(j p) -> p j", p=P), tabs[:, r, :],
                                 allow_slow_non_contiguous=True).then_inc(tabs_out, 16)
                sp.wait_ge(tabs_out, 32)
                sp.dma_start(g["tab_u"][:, :], g["tabs_d"][0:1, :]).then_inc(tabs_in, 16)
                sp.dma_start(g["tab_b0"][:, :], g["tabs_d"][1:2, :]).then_inc(tabs_in, 16)
                sp.wait_ge(tabs_in, 32)
                sp.wait_ge(dst16_out, 16)
                sp.wait_ge(sems_in, 16 * 13)

            @block.gpsimd
            def _(pool):
                pool.memset(dst_d[:, TJ - 1, :], -1).then_inc(pads, 1)
                pool.memset(nxt_d[:, TJ - 1, :], 1 << 20).then_inc(pads, 1)
                pool.memset(src_d[:, TJ - 1, :], 0).then_inc(pads, 1)
                pool.memset(xs[:, NFULL, :], 0.0).then_inc(pads, 1)
                pool.memset(g["ident"][:, :], 0.0).then_inc(id_zero, 1)
                pool.memset(g["ones"][:, :], 1.0).then_inc(consts, 1)
                pool.memset(g["eps_t"][:, :], EPS).then_inc(consts, 1)
                pool.memset(zero_row[:, :], 0.0).then_inc(consts, 1)
                pool.wait_ge(id_zero, 1)
                pool.affine_select(out=g["ident"][:, :], in_=g["ident"][:, :], compare_op=ALU.not_equal, fill=1.0,
                                   base=0, pattern=[[-1, P]], channel_multiplier=1).then_inc(consts, 1)
                pool.iota(g["node_row"][:, :], [[1, NB * W]], base=0, channel_multiplier=0,
                          allow_small_or_imprecise_dtypes=True).then_inc(consts, 1)
                for q in range(3):
                    pool.wait_ge(consts, 5 + q)
                    pool.iota(g["node_col"][W * q:W * q + W, :], [[W, NB]], base=0, channel_multiplier=1,
                              allow_small_or_imprecise_dtypes=True).then_inc(consts, 1)
                pool.wait_ge(consts, 8)
                pool.iota(unit_no[:, :], [[1, NU]], base=0, channel_multiplier=0,
                          allow_small_or_imprecise_dtypes=True).then_inc(consts, 1)
                pool.iota(step_no[:, :], [[P, 4]], base=0, channel_multiplier=1,
                          allow_small_or_imprecise_dtypes=True).then_inc(consts, 1)

            @block.vector
            def _(v):
                n = [0]

                def link(ins):
                    n[0] += 1
                    ins.then_inc(chain, 1)
                    v.wait_ge(chain, n[0])

                v.wait_ge(sems_in, 16 * 13)
                v.wait_ge(consts, 10)
                v.tensor_copy(dst_h[:, :, :], dst_d[:, :, :]).then_inc(cast, 1)
                v.tensor_copy(dst_f[:, :, :], dst_d[:, :, :]).then_inc(cast, 1)
                v.tensor_copy(src_f[:, :, :], src_d[:, :, :]).then_inc(cast, 1)
                link(v.tensor_copy(nxt_f[:, :, :], nxt_d[:, :, :]))
                v.wait_ge(cast, 3)
                link(v.tensor_tensor(nxt_f[:, :, :], dst_f[:, :, :], nxt_f[:, :, :], ALU.is_gt))
                v.tensor_reduce(uns[:, :], nxt_f[:, :, :].rearrange("p j c -> p (j c)"), AX, ALU.max
                                ).then_inc(sq, 1)
                link(v.tensor_scalar(last_b[:, :], last_i[:, :], W.bit_length() - 1, None, ALU.arith_shift_right))
                link(v.tensor_copy(key[:, :], last_b[:, :]))
                link(v.tensor_tensor(key[:, :], key[:, :], unit_no[:, :], ALU.add))
                v.memset(key[0:1, NU - 1:NU], float(NU + NB - 2)).then_inc(sq, 1)
                v.wait_ge(turned, 1)
                link(v.tensor_scalar(flag[:, :], ps[1][:, 0:1], 1.0, None, ALU.min))
                link(v.tensor_scalar(keep[:, :], flag[:, :], -1.0, 1.0, ALU.mult, ALU.add))
                for j in range(4):
                    link(v.tensor_scalar(junk[:, :], ps[0][:, 0:NU], step_no[:, j:j + 1], 0.0, ALU.is_lt, ALU.add,
                                         accum_out=cnt[:, j:j + 1]))
                link(v.tensor_tensor(stair_b[:, :], step_no[:, :], cnt[:, :], ALU.subtract))
                link(v.tensor_scalar(stair_b[:, :], stair_b[:, :], float(NB - 1), keep[:, 0:1], ALU.min, ALU.mult))
                link(v.tensor_copy(tabs[:, 1, :], stair_b[:, :]))
                link(v.tensor_scalar(lin[:, :], step_no[:, :], float(NU), flag[:, 0:1], ALU.min, ALU.mult))
                link(v.tensor_scalar(tmp4[:, :], cnt[:, :], keep[:, 0:1], None, ALU.mult))
                link(v.tensor_tensor(tu[:, :], tmp4[:, :], lin[:, :], ALU.add))
                v.tensor_copy(tabs[:, 0, :], tu[:, :]).then_inc(step_ready, 1)
                v.tensor_scalar(g["flag_row"][:, :], zero_row[:, :], flag[0:1, 0:1], None, ALU.add).then_inc(sq, 1)
                v.tensor_scalar(g["n_pass_t"][:, :], flag[0:1, 0:1], float(NB - 1), 1.0, ALU.mult, ALU.add
                                ).then_inc(sq, 1)
                for j in range(TJ):
                    hold(v, turned, 2 + 2 * j)
                    v.tensor_copy(dst_t[:, P * j:P * j + P], ps[2][:, 0:P]).then_inc(copied, 1)
                    hold(v, turned, 3 + 2 * j)
                    v.tensor_copy(src_t[:, P * j:P * j + P], ps[3][:, 0:P]).then_inc(copied, 1)

            @block.tensor
            def _(pe):
                pe.wait_ge(consts, 10)
                pe.wait_ge(sq, 2)
                pe.matmul(ps[0][:, 0:NU], g["ones"][0:1, :], key[:, :], start=True, stop=True)
                pe.matmul(ps[1][:, 0:1], g["ones"][:, :], uns[:, :], start=True, stop=True).then_inc(turned, 1)
                pe.wait_ge(cast, 3)
                for j in range(TJ):
                    if j:
                        hold(pe, copied, 2 * j - 1)
                    pe.transpose(ps[2][:, 0:P], dst_f[:, j, :], g["ident"][:, :]).then_inc(turned, 1)
                    if j:
                        hold(pe, copied, 2 * j)
                    pe.transpose(ps[3][:, 0:P], src_f[:, j, :], g["ident"][:, :]).then_inc(turned, 1)


def hold(eng, semaphore, value, gate=None):
    if isinstance(value, int) and value <= 0:
        return
    eng.wait_ge(semaphore, value)
    if gate is not None:
        eng.sem_inc(gate)


def turns(eng, body):
    body(0)
    with eng.Fori(1, NT // UT) as g:
        body(g)


def row_bc(ap, n):
    return ap.unsqueeze(2).to_broadcast([ap.shape[0], ap.shape[1], n])


def center(v, link, src3, dst3, sq3, mean):
    link(v.tensor_reduce(mean[:, :], src3[:, :, :], AX, ALU.add))
    link(v.tensor_scalar(mean[:, :], mean[:, :], 1.0 / D, None, ALU.mult))
    link(v.tensor_tensor(dst3[:, :, :], src3[:, :, :], row_bc(mean[:, :], D), ALU.subtract))


def load_weights(sp, w, layer, done):
    l1 = bass.ds(layer, 1)
    loads = [
        (w["wlr"][:, 0:HD], w["Wl"][l1].rearrange("l d f -> (l d) f")),
        (w["wlr"][:, HD:2 * HD], w["Wr"][l1].rearrange("l d f -> (l d) f")),
        (w["blr"][:, 0:HD], w["bl"][l1].rearrange("l f -> (l f)").partition_broadcast(P)),
        (w["blr"][:, HD:2 * HD], w["br"][l1].rearrange("l f -> (l f)").partition_broadcast(P)),
        (w["att_row"][:, :], w["att"][l1].rearrange("l h f -> (l h f)").partition_broadcast(P)),
        (w["pb_row"][:, :], w["proj_b"][l1].rearrange("l f -> (l f)").partition_broadcast(P)),
        (w["b2_row"][:, :], w["b2"][l1].rearrange("l f -> (l f)").partition_broadcast(P)),
        (w["w1"][:, :], w["W1"][l1].rearrange("l d f -> (l d) f")),
        (w["pw"][:, :, :], w["proj_W"][l1].rearrange("l (h f) d -> f (l h) d", h=H)),
        (w["w2"][:, :, :], w["W2"][l1].rearrange("l (c f) d -> f (l c) d", f=P)),
        (w["gat_col"][:, :], w["gat_b"][l1].rearrange("l (h f) -> f (l h)", h=H)),
        (w["b1_col"][:, :], w["b1"][l1].rearrange("l (c f) -> f (l c)", f=P)),
    ] + [(w["gcol"][:, i:i + 1], w[k][l1].rearrange("l f -> f l"))
         for i, k in enumerate(("ln1_g", "ln1_b", "ln2_g", "ln2_b"))]
    for to, of in loads:
        sp.dma_start(to, of, allow_slow_non_contiguous=True).then_inc(done, 16)
    return 16 * len(loads)


def project_nodes(nc, sb, sem, ps, w, s, layer):
    weights_in = sem("weights_in")
    chain = sem("chain")
    centered = sem("centered")
    squared = sem("squared")
    var_ready = sem("var_ready")
    std_ready = sem("std_ready")
    xn_ready = sem("xn_ready")
    xn_turned = sem("xn_turned")
    h_ready = sem("h_ready")
    proj_ready = sem("proj_ready")
    proj_read = sem("proj_read")
    xr_ready = sem("xr_ready")
    hi_ready = sem("hi_ready")
    rest_ready = sem("rest_ready")
    mid_ready = sem("mid_ready")
    row_ready = sem("row_ready")
    split_ready = sem("split_ready")
    row_out = [sem(f"row_out{i}") for i in range(UT)]
    split_out = [sem(f"split_out{i}") for i in range(UT)]
    xr3_in = sem("xr3_in")
    state = sem("state")
    link_s = sem("link_s")
    var = sb("var", [P, NT], F32)
    sq = sb("sq", [P, NT, P], F32)
    xn = sb("xn", [P, UT, P], F32)
    hT = sb("hT", [P, UT, P], F32)
    row = sb("row", [P, UT, H, RC], F32)
    xrf = sb("xrf", [P, UT, XC], F32)
    rest = sb("rest", [P, UT, XC], F32)
    split = sb("split", [P, UT, 3, XC], BF16)
    xs, xc, mean, rstd = s["xs"], s["xc"], s["mean"], s["rstd"]
    NWTS = 16 * 16
    bank_t = [0, 1, 2, 0, 1]
    bank_p = [3, 4, 5, 3, 4]

    with nc.Block() as block:
        @block.sync
        def _(sp):
            assert load_weights(sp, w, layer, weights_in) == NWTS
            @partial(turns, sp)
            def _(g):
                for k in range(UT):
                    i = g * UT + k
                    hold(sp, row_ready, i + 1, link_s)
                    sp.dma_start(s["table"][bass.ds(i * P, P), :], row[:, k, :, :].rearrange("p h c -> p (h c)")
                                 ).then_inc(row_out[k], 16)
                    hold(sp, split_ready, i + 1, link_s)
                    sp.dma_start(s["xr_split"][:, bass.ds(i * P, P), :].rearrange("q n c -> n q c"),
                                 split[:, k, :, :]).then_inc(split_out[k], 16)
            for k in range(UT):
                sp.wait_ge(row_out[k], 16 * (NT // UT))
                sp.wait_ge(split_out[k], 16 * (NT // UT))
            for q in range(3):
                sp.dma_start(s["xr3"][W * q:W * q + W, :, :],
                             s["xr_split"][q, 0:NB * W, :].rearrange("(b j) c -> j b c", j=W)).then_inc(xr3_in, 16)
            sp.wait_ge(xr3_in, 48)
            sp.wait_ge(weights_in, NWTS)

        @block.gpsimd
        def _(pool):
            pool.memset(s["acc"][:, :, :], 0.0).then_inc(state, 1)
            pool.memset(s["run_max"][:, :], FLOOR).then_inc(state, 1)
            pool.memset(row[:, :, :, D:D + 1], 1.0).then_inc(state, 1)
            pool.tensor_copy(s["tab_b"][:, :], s["tab_b0"][:, :]).then_inc(state, 1)

        @block.vector
        def _(v):
            n = [0]

            def link(ins):
                n[0] += 1
                ins.then_inc(chain, 1)
                v.wait_ge(chain, n[0])

            center(v, link, xs, xc, sq, mean)
            v.tensor_copy(mean[:, 0:1], mean[:, 0:1]).then_inc(centered, 1)
            v.wait_ge(squared, 1)
            v.tensor_reduce(var[:, :], sq[:, :, :], AX, ALU.add).then_inc(var_ready, 1)
            v.wait_ge(std_ready, 1)
            link(v.reciprocal(rstd[:, :], rstd[:, :]))
            v.wait_ge(weights_in, NWTS)
            v.wait_ge(state, 4)
            base = n[0]
            @partial(turns, v)
            def _(g):
                for k in range(UT):
                    i = g * UT + k
                    v.tensor_scalar(xn[:, k, :], xc[:, bass.ds(i, 1), :].rearrange("p a d -> p (a d)"),
                                    rstd[:, bass.ds(i, 1)], None, ALU.mult).then_inc(xn_ready, 1)
                for k in range(UT):
                    i = g * UT + k
                    hold(v, proj_ready, i + 1)
                    pp = ps[bank_p[k]]
                    hold(v, row_out[k], g * 16)
                    v.tensor_tensor(row[:, k, :, 0:D], pp[:, 0:HD].rearrange("p (h d) -> p h d", h=H),
                                    w["blr"][:, 0:HD].rearrange("p (h d) -> p h d", h=H), ALU.add
                                    ).then_inc(proj_read, 1)
                    hold(v, mid_ready, g * UT)
                    v.tensor_tensor(xrf[:, k, 0:HD], pp[:, HD:2 * HD], w["blr"][:, HD:2 * HD], ALU.add
                                    ).then_inc(proj_read, 1)
                    hold(v, proj_read, 2 * i + 2)
                    for h in range(H):
                        a = w["att_row"][:, h * D:h * D + D]
                        r1 = v.tensor_tensor_reduce(sq[:, 2 * H * k + h, :], row[:, k, h, 0:D], a, SLOPE, 0.0, ALU.mult, ALU.add,
                                                    row[:, k, h, D + 1:D + 2])
                        r1.then_inc(row_ready, 1) if h == H - 1 else r1.then_inc(link_s, 1)
                        r2 = v.tensor_tensor_reduce(sq[:, 2 * H * k + H + h, :], xrf[:, k, h * D:h * D + D], a, SLOPE, 0.0, ALU.mult,
                                                    ALU.add, xrf[:, k, HD + h:HD + h + 1])
                        r2.then_inc(xr_ready, 1)
                for k in range(UT):
                    i = g * UT + k
                    hold(v, hi_ready, i + 1)
                    v.tensor_tensor(rest[:, k, :], xrf[:, k, :], split[:, k, 0, :], ALU.subtract
                                    ).then_inc(rest_ready, 1)
                for k in range(UT):
                    i = g * UT + k
                    hold(v, mid_ready, i + 1)
                    v.tensor_tensor(split[:, k, 2, :], rest[:, k, :], split[:, k, 1, :], ALU.subtract
                                    ).then_inc(split_ready, 1)

        @block.scalar
        def _(act):
            act.wait_ge(centered, 1)
            act.activation(sq[:, :, :], xc[:, :, :], ACT.Square).then_inc(squared, 1)
            act.wait_ge(var_ready, 1)
            act.activation(rstd[:, :], var[:, :], ACT.Sqrt, bias=s["eps_t"][:, 0:1], scale=1.0 / D
                           ).then_inc(std_ready, 1)
            act.wait_ge(weights_in, NWTS)
            @partial(turns, act)
            def _(g):
                for k in range(UT):
                    i = g * UT + k
                    hold(act, xn_turned, i + 1)
                    hold(act, proj_ready, g * UT) if k == 0 else None
                    act.activation(hT[:, k, :], ps[bank_t[k]][:, 0:P], ACT.Identity, bias=w["gcol"][:, 1:2],
                                   scale=w["gcol"][:, 0:1]).then_inc(h_ready, 1)
                for k in range(UT):
                    i = g * UT + k
                    hold(act, xr_ready, 2 * i + 2)
                    hold(act, split_out[k], g * 16)
                    act.copy(split[:, k, 0, :], xrf[:, k, :]).then_inc(hi_ready, 1)
                for k in range(UT):
                    i = g * UT + k
                    hold(act, rest_ready, i + 1)
                    act.copy(split[:, k, 1, :], rest[:, k, :]).then_inc(mid_ready, 1)

        @block.tensor
        def _(pe):
            pe.wait_ge(weights_in, NWTS)
            @partial(turns, pe)
            def _(g):
                for k in range(UT + 1):
                    if k < UT:
                        i = g * UT + k
                        hold(pe, xn_ready, i + 1)
                        if k in (0, 1, 3, 4):
                            hold(pe, h_ready, (g * UT + k - 1) if k else g * UT)
                        pe.transpose(ps[bank_t[k]][:, 0:P], xn[:, k, :], s["ident"][:, :]).then_inc(xn_turned, 1)
                    if k:
                        j = k - 1
                        i = g * UT + j
                        hold(pe, h_ready, i + 1)
                        hold(pe, proj_read, 2 * i if j == 0 else 2 * (i - 1))
                        pe.matmul(ps[bank_p[j]][:, :], hT[:, j, :], w["wlr"][:, :], start=True, stop=True
                                  ).then_inc(proj_ready, 1)


def edge_pass(nc, sb, sem, ps, s):
    rows_in = [sem(f"rows_in{i}") for i in range(RING)]
    idx_ready = sem("idx_ready")
    dstb_in = [sem(f"dstb_in{i}") for i in range(RING)]
    dstb_used = sem("dstb_used")
    oh_ready = sem("oh_ready")
    z_ready = sem("z_ready")
    relu_done = sem("relu_done")
    dots_done = sem("dots_done")
    outside_ready = sem("outside_ready")
    score_ready = sem("score_ready")
    masked = sem("masked")
    top_ready = sem("top_ready")
    top_turned = sem("top_turned")
    unit_max = sem("unit_max")
    new_max = sem("new_max")
    drop_ready = sem("drop_ready")
    max_saved = sem("max_saved")
    max_spread = sem("max_spread")
    shifted = sem("shifted")
    weights_ready = sem("weights_ready")
    sums_ready = sem("sums_ready")
    merged = sem("merged")
    gate = sem("gate")
    tab_next = sem("tab_next")

    rows = sb("rows", [P, RING, K, H, RC], F32)
    idx = sb("idx", [P, RING, K], I32)
    dstb = sb("dstb", [3 * W, RING, UE], I16)
    oh = sb("oh", [3 * W, 2, UE], BF16)
    rz = sb("rz", [P, 2, K * HD], F32)
    dots = sb("dots", [P, 2, K * H], F32)
    score = sb("score", [P, 2, K * H], F32)
    outside = sb("outside", [P, K * H, W], F32)
    msc = sb("msc", [P, 2, K * H, W], F32)
    top = sb("top", [P, HW], F32)
    umax = sb("umax", [HW, 1], F32)
    nmax = sb("nmax", [HW, 2, 1], F32)
    drop = sb("drop", [HW, 2, 1], F32)
    dmax = sb("dmax", [P, 2, K * HW], F32)
    wgt = sb("wgt", [P, 2, K, HW], F32)
    decay = sb("decay", [HW, RING, 1], F32)
    BZ, BR, BT, BS = (0, 1), (2, 3), 4, (5, 6)
    att8 = s["att8"] if "att8" in s else None
    acc, run_max = s["acc"], s["run_max"]

    def once(k, first, i):
        return not (first and k < 0)

    with nc.Block() as block:
        def load(eng, tab, at, n):
            return eng.value_load(s[tab][0:1, bass.ds(at, 1)], min_val=0, max_val=n)

        def pass_ticks(eng, tick, lag):
            for k in range(RING):
                tick(k, k)
            with eng.Fori(1, GROUPS) as g:
                for k in range(RING):
                    tick(k, g * RING + k)
            for k in range(lag):
                tick(k, NS + k)

        def runs(i, lag):
            return not isinstance(i, int) or 0 <= i - lag < NS

        @block.gpsimd
        def _(pool):
            def tick(k, i):
                u = load(pool, "tab_u", i, NU)
                hold(pool, sums_ready, i - RING + 1, gate)
                pool.tensor_copy(idx[:, k, :], s["src_t"][:, bass.ds(u * K, K)]).then_inc(idx_ready, 1)
                hold(pool, idx_ready, i + 1, gate)
                for t in range(K):
                    pool.indirect_dma_start(rows[:, k, t, :, :].rearrange("p h c -> p (h c)"), None,
                                            s["table"][:, :],
                                            bass.IndirectOffsetOnAxis(ap=idx[:, k, t:t + 1], axis=0)
                                            ).then_inc(rows_in[k], 16)
            pass_ticks(pool, tick, 0)
            for k in range(RING):
                pool.wait_ge(rows_in[k], 16 * K * GROUPS)

        @block.sync
        def _(sp):
            def tick(k, i):
                u = load(sp, "tab_u", i, NU)
                hold(sp, oh_ready, i - RING + 1, gate)
                sp.dma_start(dstb[:, k, :], s["dst16"][bass.ds(u * UE, UE)].partition_broadcast(3 * W)
                             ).then_inc(dstb_in[k], 16)
            pass_ticks(sp, tick, 1)

        @block.tensor
        def _(pe):
            def turn_top(i):
                if runs(i, 2):
                    j = i - 2
                    hold(pe, top_ready, j + 1, gate)
                    hold(pe, shifted, j, gate)
                    pe.transpose(ps[BT][0:HW, 0:P], top[:, :], s["ident"][:, :]).then_inc(top_turned, 1)

            def add_rows(k, i):
                if runs(i, 0):
                    b = load(pe, "tab_b", i, NB - 1)
                    hold(pe, rows_in[k], (i // RING if isinstance(i, int) else pe_g[0]) * 16 * K + 16 * K)
                    hold(pe, oh_ready, i + 1)
                    hold(pe, score_ready, i - 1)
                    z, lin = ps[BZ[k % 2]], ps[BR[k % 2]]
                    xr_b = s["xr3"][:, bass.ds(b, 1), :].rearrange("p a c -> p (a c)")
                    for t in range(K):
                        sel = oh[:, k % 2, t * P:t * P + P]
                        pe.matmul(z[:, t * HD:t * HD + HD], sel, xr_b[:, 0:HD], start=(t == 0), stop=False)
                        m = pe.matmul(lin[:, t * H:t * H + H], sel, xr_b[:, HD:XC], start=(t == 0), stop=(t == K - 1))
                        m.then_inc(dstb_used, 1) if t == K - 1 else None
                    for t in range(K):
                        m = pe.matmul(z[:, t * HD:t * HD + HD], s["ident"][:, :], rows[:, k, t, :, 0:D],
                                      start=False, stop=(t == K - 1))
                    m.then_inc(z_ready, 1)

            def spread_max(k, i):
                if runs(i, 2):
                    j = i - 2
                    hold(pe, new_max, j + 1, gate)
                    pe.transpose(ps[BT][:, P:P + HW], nmax[:, k % 2, :].to_broadcast([HW, P]),
                                 s["ident"][0:HW, 0:HW]).then_inc(max_spread, 1)

            def sum_rows(k, i):
                if runs(i, 3):
                    j = i - 3
                    hold(pe, weights_ready, j + 1)
                    hold(pe, merged, j - 1)
                    kk = (k - 3) % RING
                    out = ps[BS[kk % 2]]
                    for t in range(K):
                        for h in range(H):
                            m = pe.matmul(out[h * W:h * W + W, 0:D + 1], wgt[:, kk % 2, t, h * W:h * W + W],
                                          rows[:, kk, t, h, 0:D + 1], start=(t == 0), stop=(t == K - 1))
                    m.then_inc(sums_ready, 1)

            pe_g = [0]

            def tick(k, i):
                turn_top(i)
                add_rows(k, i)
                spread_max(k, i)
                sum_rows(k, i)

            for k in range(RING):
                tick(k, k)
            with pe.Fori(1, GROUPS) as g:
                pe_g[0] = g
                for k in range(RING):
                    tick(k, g * RING + k)
            for k in range(LAG):
                tick(k, NS + k)

        @block.scalar
        def _(act):
            def tick(k, i):
                if runs(i, 0):
                    hold(act, z_ready, i + 1)
                    hold(act, dots_done, i - 1)
                    act.activation(rz[:, k % 2, :], ps[BZ[k % 2]][:, 0:K * HD], ACT.Relu).then_inc(relu_done, 1)
                if runs(i, 2):
                    j = i - 2
                    kk = (k - 2) % RING
                    hold(act, shifted, j + 1)
                    hold(act, sums_ready, j - 1)
                    act.activation(decay[:, kk, :], drop[:, kk % 2, :], ACT.Exp)
                    act.activation(wgt[:, kk % 2, :, :].rearrange("p t c -> p (t c)"), dmax[:, kk % 2, :], ACT.Exp
                                   ).then_inc(weights_ready, 1)
            pass_ticks(act, tick, 2)

        @block.vector
        def _(v):
            def one_hot(k, i):
                b = load(v, "tab_b", i, NB - 1)
                hold(v, dstb_in[k], 16 * grp(i) + 16)
                hold(v, dstb_used, i - 1)
                v.tensor_scalar(oh[:, k % 2, :], dstb[:, k, :], s["node_col"][:, bass.ds(b, 1)], None,
                                ALU.is_equal).then_inc(oh_ready, 1)

            group = [0]

            def grp(i):
                return i // RING if isinstance(i, int) else group[0]

            def maximum(k, i):
                if runs(i, 2):
                    j, p = i - 2, k % 2
                    b = load(v, "tab_b", j, NB - 1)
                    hold(v, top_turned, j + 1)
                    v.tensor_reduce(umax[:, :], ps[BT][0:HW, 0:P], AX, ALU.max).then_inc(unit_max, 1)
                    hold(v, unit_max, j + 1)
                    hold(v, max_saved, j)
                    rm = run_max[:, bass.ds(b, 1)]
                    v.tensor_tensor(nmax[:, p, :], rm, umax[:, :], ALU.max).then_inc(new_max, 1)
                    hold(v, new_max, j + 1)
                    hold(v, weights_ready, j - 1)
                    v.tensor_tensor(drop[:, p, :], rm, nmax[:, p, :], ALU.subtract).then_inc(drop_ready, 1)
                    hold(v, drop_ready, j + 1)
                    v.tensor_scalar(rm, nmax[:, p, :], 1.0, None, ALU.mult).then_inc(max_saved, 1)

            def dot(k, i):
                if runs(i, 1):
                    j, p = i - 1, (k - 1) % 2
                    kk = (k - 1) % RING
                    hold(v, relu_done, j + 1)
                    for t in range(K):
                        for h in range(H):
                            c = t * H + h
                            m = v.tensor_tensor_reduce(rz[:, p, c * D:c * D + D], rz[:, p, c * D:c * D + D],
                                                       s["att_row"][:, h * D:h * D + D], 1.0 - SLOPE,
                                                       rows[:, kk, t, h, D + 1:D + 2], ALU.mult, ALU.add,
                                                       dots[:, p, c:c + 1])
                    m.then_inc(dots_done, 1)

            def shift(k, i):
                if runs(i, 2):
                    j, p = i - 2, k % 2
                    hold(v, max_spread, j + 1)
                    v.tensor_tensor(dmax[:, p, :].rearrange("p (t c) -> p t c", t=K),
                                    msc[:, p, :, :].rearrange("p (t h) w -> p t (h w)", t=K),
                                    ps[BT][:, P:P + HW].unsqueeze(1).to_broadcast([P, K, HW]), ALU.subtract
                                    ).then_inc(shifted, 1)

            def mask(k, i):
                if runs(i, 1):
                    j, p = i - 1, (k - 1) % 2
                    b = load(v, "tab_b", j, NB - 1)
                    u = load(v, "tab_u", j, NU)
                    hold(v, masked, j)
                    v.tensor_tensor(outside[:, :, :].rearrange("p (t h) w -> p t (h w)", t=K)
                                    if False else outside[:, :, :].rearrange("p (t h) w -> p t h w", t=K),
                                    s["node_row"][:, bass.ds(b * W, W)].unsqueeze(1).unsqueeze(1)
                                    .to_broadcast([P, K, H, W]),
                                    s["dst_t"][:, bass.ds(u * K, K)].unsqueeze(2).unsqueeze(3)
                                    .to_broadcast([P, K, H, W]), ALU.not_equal).then_inc(outside_ready, 1)
                    hold(v, dots_done, j + 1)
                    v.tensor_tensor(score[:, p, :], dots[:, p, :], ps[BR[p]][:, 0:K * H], ALU.add
                                    ).then_inc(score_ready, 1)
                    hold(v, score_ready, j + 1)
                    hold(v, outside_ready, j + 1)
                    v.scalar_tensor_tensor(msc[:, p, :, :], outside[:, :, :], -MASK,
                                           score[:, p, :].unsqueeze(2).to_broadcast([P, K * H, W]),
                                           ALU.mult, ALU.add).then_inc(masked, 1)
                    hold(v, masked, j + 1)
                    m4 = msc[:, p, :, :].rearrange("p (t h) w -> p t (h w)", t=K)
                    hold(v, top_turned, j)
                    v.tensor_tensor(top[:, :], m4[:, 0, :], m4[:, 1, :], ALU.max).then_inc(top_ready, 1)

            def merge(k, i):
                if runs(i, 4):
                    j, kk = i - 4, (k - 4) % RING
                    b = load(v, "tab_b", j, NB - 1)
                    hold(v, sums_ready, j + 1)
                    hold(v, merged, j)
                    a = acc[:, bass.ds(b, 1), :].rearrange("p a c -> p (a c)")
                    v.scalar_tensor_tensor(a, a, decay[:, kk, :], ps[BS[kk % 2]][0:HW, 0:D + 1], ALU.mult, ALU.add
                                           ).then_inc(merged, 1)

            def tick(k, i):
                maximum(k, i)
                if isinstance(i, int) and i == 0:
                    one_hot(0, 0)
                nxt = i + 1
                if isinstance(i, int):
                    if nxt < NS:
                        group[0] = nxt // RING
                        one_hot((k + 1) % RING, nxt)
                else:
                    if k == RING - 1:
                        one_hot_last(nxt)
                    else:
                        one_hot(k + 1, nxt)
                dot(k, i)
                shift(k, i)
                mask(k, i)
                merge(k, i)

            def one_hot_last(nxt):
                group[0] = group[0] + 1
                one_hot(0, nxt)
                group[0] = group[0] - 1

            for k in range(RING):
                tick(k, k)
            with v.Fori(1, GROUPS) as g:
                for k in range(RING):
                    group[0] = g
                    tick(k, g * RING + k)
            for k in range(LAG + 1):
                tick(k, NS + k)
            v.tensor_tensor(s["tab_b"][:, :], s["tab_b"][:, :], s["flag_row"][:, :], ALU.add).then_inc(tab_next, 1)


def update_nodes(nc, sb, sem, ps, w, s):
    chain = sem("chain")
    att_ready = sem("att_ready")
    att_turned = sem("att_turned")
    gt_ready = sem("gt_ready")
    proj_ready = sem("proj_ready")
    x_ready = sem("x_ready")
    centered = sem("centered")
    squared = sem("squared")
    var_ready = sem("var_ready")
    std_ready = sem("std_ready")
    xn_ready = sem("xn_ready")
    xn_turned = sem("xn_turned")
    h_ready = sem("h_ready")
    up_ready = sem("up_ready")
    gelu_ready = sem("gelu_ready")
    down_ready = sem("down_ready")
    y_ready = sem("y_ready")
    link_s = sem("link_s")
    q = P // W
    gT = sb("gT", [P, UT, H, P], F32)
    rden = sb("rden", [HW, NBP], F32)
    sq = sb("sq", [P, NT, P], F32)
    var = sb("var", [P, NT], F32)
    xn = sb("xn", [P, UT, P], F32)
    hT = sb("hT", [P, UT, P], F32)
    ge = sb("ge", [P, UT, MLP // P, P], F32)
    an = ge[0:HW, :, 0:q, :]
    tmp = sb("tmp", [P, UT, P], F32)
    xs, xc, mean, rstd, acc = s["xs"], s["xc"], s["mean"], s["rstd"], s["acc"]
    bank = [0, 1, 2, 0, 1]
    bank2 = [3, 4, 5, 3, 4]
    bank3 = [6, 7, 6, 7, 6]

    def tile(ap, i):
        return ap[:, bass.ds(i, 1), :].rearrange("p a d -> p (a d)")

    with nc.Block() as block:
        @block.vector
        def _(v):
            n = [0]

            def link(ins):
                n[0] += 1
                ins.then_inc(chain, 1)
                v.wait_ge(chain, n[0])

            link(v.tensor_scalar(rden[:, :], acc[:, :, D], 1e-16, None, ALU.add))
            link(v.reciprocal(rden[:, :], rden[:, :]))
            @partial(turns, v)
            def _(g):
                for k in range(UT):
                    i = g * UT + k
                    v.tensor_tensor(an[:, k, :, :], acc[:, bass.ds(i * q, q), 0:D],
                                    row_bc(rden[:, bass.ds(i * q, q)], D), ALU.mult).then_inc(att_ready, 1)
                for k in range(UT):
                    i = g * UT + k
                    hold(v, proj_ready, i + 1)
                    v.tensor_tensor(tmp[:, k, :], ps[bank2[k]][:, 0:P], w["pb_row"][:, :], ALU.add
                                    ).then_inc(y_ready, 1)
                    hold(v, y_ready, i + 1)
                    v.tensor_tensor(tile(xs, i), tile(xs, i), tmp[:, k, :], ALU.add).then_inc(x_ready, 1)
            v.wait_ge(x_ready, NT)
            center(v, link, xs, xc, sq, mean)
            v.tensor_copy(mean[:, 0:1], mean[:, 0:1]).then_inc(centered, 1)
            v.wait_ge(squared, 1)
            v.tensor_reduce(var[:, :], sq[:, :, :], AX, ALU.add).then_inc(var_ready, 1)
            v.wait_ge(std_ready, 1)
            link(v.reciprocal(rstd[:, :], rstd[:, :]))
            @partial(turns, v)
            def _(g):
                for k in range(UT):
                    i = g * UT + k
                    v.tensor_scalar(xn[:, k, :], tile(xc, i), rstd[:, bass.ds(i, 1)], None, ALU.mult
                                    ).then_inc(xn_ready, 1)
                for k in range(UT):
                    i = g * UT + k
                    hold(v, down_ready, i + 1)
                    v.tensor_tensor(tmp[:, k, :], ps[bank3[k]][:, 0:P], w["b2_row"][:, :], ALU.add
                                    ).then_inc(y_ready, 1)
                    hold(v, y_ready, NT + i + 1)
                    v.tensor_tensor(tile(xs, i), tile(xs, i), tmp[:, k, :], ALU.add).then_inc(x_ready, 1)

        @block.scalar
        def _(act):
            @partial(turns, act)
            def _(g):
                for k in range(UT):
                    i = g * UT + k
                    hold(act, att_turned, i + 1)
                    if k == 0:
                        hold(act, proj_ready, g * UT)
                    t4 = ps[bank[k]][:, 0:q * HW].rearrange("p (q h w) -> p q h w", q=q, h=H)
                    for h in range(H):
                        act.activation(gT[:, k, h, :].rearrange("p (q w) -> p q w", q=q), t4[:, :, h, :],
                                       ACT.Identity, bias=w["gat_col"][:, h:h + 1]).then_inc(gt_ready, 1)
            act.wait_ge(centered, 1)
            act.activation(sq[:, :, :], xc[:, :, :], ACT.Square).then_inc(squared, 1)
            act.wait_ge(var_ready, 1)
            act.activation(rstd[:, :], var[:, :], ACT.Sqrt, bias=s["eps_t"][:, 0:1], scale=1.0 / D
                           ).then_inc(std_ready, 1)
            @partial(turns, act)
            def _(g):
                for k in range(UT):
                    i = g * UT + k
                    hold(act, xn_turned, i + 1)
                    act.activation(hT[:, k, :], ps[bank[k]][:, 0:P], ACT.Identity, bias=w["gcol"][:, 3:4],
                                   scale=w["gcol"][:, 2:3]).then_inc(h_ready, 1)
                for k in range(UT):
                    i = g * UT + k
                    hold(act, up_ready, i + 1)
                    if k == 0:
                        hold(act, down_ready, g * UT)
                    for c in range(MLP // P):
                        m = act.activation(ge[:, k, c, :], ps[bank2[k]][:, c * P:c * P + P], ACT.Gelu_apprx_tanh,
                                           bias=w["b1_col"][:, c:c + 1])
                    m.then_inc(gelu_ready, 1)

        @block.tensor
        def _(pe):
            @partial(turns, pe)
            def _(g):
                for k in range(UT):
                    i = g * UT + k
                    hold(pe, att_ready, i + 1, link_s)
                    hold(pe, gt_ready, 2 * g * UT + 2 * max(k - 1, 0), link_s)
                    for j in range(q):
                        m = pe.transpose(ps[bank[k]][:, j * HW:j * HW + HW], an[:, k, j, :],
                                         s["ident"][0:HW, 0:HW])
                    m.then_inc(att_turned, 1)
                for k in range(UT):
                    i = g * UT + k
                    hold(pe, gt_ready, 2 * i + 2)
                    hold(pe, y_ready, g * UT + max(k - 1, 0))
                    for h in range(H):
                        m = pe.matmul(ps[bank2[k]][:, 0:P], gT[:, k, h, :], w["pw"][:, h, :], start=(h == 0),
                                      stop=(h == H - 1))
                    m.then_inc(proj_ready, 1)
            pe.wait_ge(x_ready, NT)
            @partial(turns, pe)
            def _(g):
                for k in range(UT):
                    i = g * UT + k
                    hold(pe, xn_ready, i + 1)
                    hold(pe, h_ready, g * UT + max(k - 1, 0))
                    pe.transpose(ps[bank[k]][:, 0:P], xn[:, k, :], s["ident"][:, :]).then_inc(xn_turned, 1)
                for k in range(UT + 1):
                    if k < UT:
                        i = g * UT + k
                        hold(pe, h_ready, i + 1)
                        hold(pe, gelu_ready, g * UT + max(k - 1, 0))
                        for c in range(MLP // P):
                            m = pe.matmul(ps[bank2[k]][:, c * P:c * P + P], w["w1"][:, c * P:c * P + P],
                                          hT[:, k, :], start=True, stop=True)
                        m.then_inc(up_ready, 1)
                    if k:
                        j = k - 1
                        i = g * UT + j
                        hold(pe, gelu_ready, i + 1)
                        hold(pe, y_ready, NT + g * UT + max(j - 1, 0))
                        for c in range(MLP // P):
                            m = pe.matmul(ps[bank3[j]][:, 0:P], ge[:, j, c, :], w["w2"][:, c, :], start=(c == 0),
                                          stop=(c == MLP // P - 1))
                        m.then_inc(down_ready, 1)


def finish(nc, sb, sem, ps, s, x, out):
    chain = sem("chain")
    x_in = sem("x_in")
    centered = sem("centered")
    squared = sem("squared")
    var_ready = sem("var_ready")
    std_ready = sem("std_ready")
    y_ready = sem("y_ready")
    stored = sem("stored")
    x0 = sb("x0", [P, NT, P], F32)
    sq = sb("sq", [P, NT, P], F32)
    var = sb("var", [P, NT], F32)
    xs, xc, mean, rstd = s["xs"], s["xc"], s["mean"], s["rstd"]
    F = N // P
    with nc.Block() as block:
        @block.sync
        def _(sp):
            sp.dma_start(x0[:, 0:F, :], x[0:F * P, :].rearrange("(t p) d -> p t d", p=P)).then_inc(x_in, 16)
            sp.dma_start(x0[0:N - F * P, F, :], x[F * P:N, :]).then_inc(x_in, 16)
            sp.wait_ge(y_ready, 1)
            sp.dma_start(out[0:F * P, :].rearrange("(t p) d -> p t d", p=P), sq[:, 0:F, :]).then_inc(stored, 16)
            sp.dma_start(out[F * P:N, :], sq[0:N - F * P, F, :]).then_inc(stored, 16)
            sp.wait_ge(stored, 32)

        @block.vector
        def _(v):
            n = [0]

            def link(ins):
                n[0] += 1
                ins.then_inc(chain, 1)
                v.wait_ge(chain, n[0])

            v.wait_ge(x_in, 32)
            link(v.tensor_tensor(xs[:, 0:F, :], xs[:, 0:F, :], x0[:, 0:F, :], ALU.add))
            link(v.tensor_tensor(xs[0:N - F * P, F, :], xs[0:N - F * P, F, :], x0[0:N - F * P, F, :], ALU.add))
            center(v, link, xs, xc, sq, mean)
            v.tensor_copy(mean[:, 0:1], mean[:, 0:1]).then_inc(centered, 1)
            v.wait_ge(squared, 1)
            v.tensor_reduce(var[:, :], sq[:, :, :], AX, ALU.add).then_inc(var_ready, 1)
            v.wait_ge(std_ready, 1)
            link(v.reciprocal(rstd[:, :], rstd[:, :]))
            v.tensor_tensor(sq[:, :, :], xc[:, :, :], row_bc(rstd[:, :], D), ALU.mult).then_inc(y_ready, 1)

        @block.scalar
        def _(act):
            act.wait_ge(centered, 1)
            act.activation(sq[:, :, :], xc[:, :, :], ACT.Square).then_inc(squared, 1)
            act.wait_ge(var_ready, 1)
            act.activation(rstd[:, :], var[:, :], ACT.Sqrt, bias=s["eps_t"][:, 0:1], scale=1.0 / D
                           ).then_inc(std_ready, 1)


_INS = ['x', 'src', 'dst', 'L0_gnn_ln1_g', 'L0_gnn_ln1_b', 'L0_gnn_Wl', 'L0_gnn_bl', 'L0_gnn_Wr', 'L0_gnn_br',
        'L0_gnn_att', 'L0_gnn_gat_b', 'L0_gnn_proj_W', 'L0_gnn_proj_b', 'L0_gnn_ln2_g', 'L0_gnn_ln2_b', 'L0_gnn_W1',
        'L0_gnn_b1', 'L0_gnn_W2', 'L0_gnn_b2']
_OUTS = [((N, D), 'float32')]


def kernel(**inputs):
    import numpy as _np
    import concourse.bacc as _bacc
    from concourse import mybir as _mybir
    from concourse.bass_utils import run_bass_kernel_spmd as _run

    nc = _bacc.Bacc("TRN2", target_bir_lowering=False, num_devices=1)
    arrays, args = {}, []
    for name in _INS:
        a = _np.ascontiguousarray(inputs[name])
        arrays[f"in_{name}_dram"] = a
        args.append(nc.dram_tensor(f"in_{name}_dram", a.shape, _mybir.dt.from_np(a.dtype), kind="ExternalInput").ap())
    for i, (shape, dtype) in enumerate(_OUTS):
        dt = _mybir.dt.from_np(_np.dtype(dtype))
        args.append(nc.dram_tensor(f"out_{i}_dram", shape, dt, kind="ExternalOutput").ap())
    gnn(nc, *args)
    r = _run(nc, [arrays], core_ids=[0])
    got = tuple(r.results[0][f"out_{i}_dram"] for i in range(len(_OUTS)))
    return got[0]
```

```python
from contextlib import ExitStack
from functools import partial

import concourse.bass as bass
from concourse import mybir

F32 = mybir.dt.float32
BF16 = mybir.dt.bfloat16
I32 = mybir.dt.int32
I16 = mybir.dt.int16
ALU = mybir.AluOpType
ACT = mybir.ActivationFunctionType
AX = mybir.AxisListType.X

P = 128
N, D, H, L, MLP, E = 3125, 128, 2, 2, 512, 100000
HD = H * D
EPS = 1e-5
SLOPE = 0.2

K = 2
UE = K * P
NU = -(-E // UE)
W = 32
HW = H * W
NB = -(-N // W)
NT = -(-N // P)
NBP = NT * P // W
RING = 12
GROUPS = -(-(NU + NB - 1) // RING)
NS = GROUPS * RING
HALVES = GROUPS // 2 + 1
TABW = 512
TJ = -(-E // (P * P))
EFULL = (TJ - 1) * P * P
ETILES = (E - EFULL) // P
EREST = E - EFULL - ETILES * P
NUP = TJ * P // K
RC = D + 2
XC = HD + H
MASK = 2.0 ** 100
FLOOR = -1e19
FRESH = -1e20
UT = 5
assert NT % UT == 0 and GROUPS % 2 == 1 and 2 * HALVES * RING <= TABW


def gnn(nc, x, src, dst, ln1_g, ln1_b, Wl, bl, Wr, br, att, gat_b, proj_W, proj_b, ln2_g, ln2_b, W1, b1,
        W2, b2, out):
    table = nc.dram_tensor("table", (NT * P, H * RC), F32, kind="Internal").ap()
    xr_split = nc.dram_tensor("xr_split", (3, NT * P, XC), BF16, kind="Internal").ap()
    edges_d = [nc.dram_tensor(f"edges_d{i}", (NUP, UE), I32, kind="Internal").ap() for i in range(2)]
    rel_d = nc.dram_tensor("rel_d", (TABW * UE,), I16, kind="Internal").ap()
    tabs_d = nc.dram_tensor("tabs_d", (TABW,), I32, kind="Internal").ap()
    fresh_d = nc.dram_tensor("fresh_d", (TABW,), F32, kind="Internal").ap()

    with ExitStack() as ctx:
        def sb(name, shape, dt):
            return ctx.enter_context(nc.sbuf_tensor(name, shape, dt))

        ident = sb("ident", [P, P], F32)
        ones = sb("ones", [P, P], F32)
        win_col = sb("win_col", [3 * W, 1], F32)
        src_t = sb("src_t", [P, TABW, K], I32)
        rel_s = sb("rel_s", [P, TABW // P, UE], F32)
        mask_sel = sb("mask_sel", [3 * W, HW], BF16)
        fresh = sb("fresh", [HW, TABW], F32)
        tab_b = sb("tab_b", [1, TABW], I32)
        tab_b0 = sb("tab_b0", [1, TABW], I32)
        flag_row = sb("flag_row", [1, TABW], I32)
        next_w = sb("next_w", [P, 1], F32)
        back_w = sb("back_w", [P, 1], F32)
        n_pass_t = sb("n_pass_t", [1, 1], I32)
        eps_t = sb("eps_t", [P, 1], F32)
        xs = sb("xs", [P, NT, P], F32)
        mean = sb("mean", [P, NT], F32)
        rstd = sb("rstd", [P, NT], F32)
        acc = sb("acc", [HW, NBP, D + 1], F32)
        xr3 = sb("xr3", [3 * W, NB, XC], BF16)

        psum_z = [ctx.enter_context(nc.psum_tensor(f"psum{i}", [P, 512], F32)) for i in range(8)]

        sems = []

        def end_phase():
            nc.gpsimd.dma_reset(range(sems[0].num, sems[-1].num + 1))
            nc.gpsimd.sem_clear(range(sems[0].num, sems[-1].num + 1))
            nc.all_engine_barrier()
            sems.clear()

        names = [0]

        def scratch(build, *args):
            names[0] += 1
            with ExitStack() as inner:
                def sbi(name, shape, dt):
                    return inner.enter_context(nc.sbuf_tensor(f"{name}_{names[0]}", shape, dt))
                with ExitStack() as si:
                    def semi(name):
                        sems.append(si.enter_context(nc.semaphore(f"{name}_{names[0]}")))
                        return sems[-1]
                    build(nc, sbi, semi, psum_z, *args)
                    end_phase()

        scratch(setup, dict(x=x, src=src, dst=dst, edges_d=edges_d, tabs_d=tabs_d, fresh_d=fresh_d, ident=ident,
                            ones=ones, mask_sel=mask_sel, win_col=win_col, src_t=src_t, rel_s=rel_s, fresh=fresh,
                            tab_b0=tab_b0, flag_row=flag_row, next_w=next_w, back_w=back_w, n_pass_t=n_pass_t,
                            eps_t=eps_t, xs=xs))
        n_pass = nc.values_load(n_pass_t[0:1, 0:1], min_val=1, max_val=NB)

        wlr = sb("wlr", [P, 2 * HD], F32)
        blr = sb("blr", [P, 2 * HD], F32)
        att_row = sb("att_row", [P, HD], F32)
        att08 = sb("att08", [P, HD], F32)
        gcol = sb("gcol", [P, 4], F32)
        gat_col = sb("gat_col", [P, H], F32)
        b1_col = sb("b1_col", [P, 4], F32)
        pw = sb("pw", [P, H, P], F32)
        w1 = sb("w1", [P, MLP], F32)
        w2 = sb("w2", [P, MLP // P, P], F32)
        pb_row = sb("pb_row", [P, P], F32)
        b2_row = sb("b2_row", [P, P], F32)
        wts = dict(wlr=wlr, blr=blr, att_row=att_row, gcol=gcol, gat_col=gat_col, b1_col=b1_col, pw=pw, w1=w1,
                   w2=w2, pb_row=pb_row, b2_row=b2_row, Wl=Wl, Wr=Wr, bl=bl, br=br, att=att, gat_b=gat_b,
                   proj_W=proj_W, proj_b=proj_b, ln1_g=ln1_g, ln1_b=ln1_b, ln2_g=ln2_g, ln2_b=ln2_b, W1=W1, b1=b1,
                   W2=W2, b2=b2)
        st = dict(ident=ident, ones=ones, xs=xs, mean=mean, rstd=rstd, eps_t=eps_t, table=table,
                  xr_split=xr_split, xr3=xr3, acc=acc, mask_sel=mask_sel, win_col=win_col, src_t=src_t,
                  rel_s=rel_s, rel_d=rel_d, fresh=fresh, att08=att08, tab_b=tab_b,
                  tab_b0=tab_b0, flag_row=flag_row, next_w=next_w, back_w=back_w)

        with nc.Fori(0, L) as layer:
            scratch(project_nodes, wts, st, layer)
            with nc.Fori(0, n_pass) as _:
                scratch(lay_out_steps, st)
                scratch(edge_pass, st)
            scratch(update_nodes, wts, st)
        scratch(finish, st, x, out)


def setup(nc, sb, sem, ps, g):
    lists_in = sem("lists_in")
    pads = sem("pads")
    consts = sem("consts")
    id_zero = sem("id_zero")
    rows_out = sem("rows_out")
    marks = sem("marks")
    spread = sem("spread")
    units_ready = sem("units_ready")
    steps_in = sem("steps_in")
    src_cast = sem("src_cast")
    turned = sem("turned")
    copied = sem("copied")
    tabs_ready = sem("tabs_ready")
    chain = sem("chain")
    tabs_out = sem("tabs_out")
    tabs_in = sem("tabs_in")
    J = TABW // P

    dst_d = sb("dst_d", [P, TJ, P], I32)
    nxt_d = sb("nxt_d", [P, TJ, P], I32)
    src_d = sb("src_d", [P, TJ, P], I32)
    dst_f = sb("dst_f", [P, TJ, P], F32)
    nxt_f = sb("nxt_f", [P, TJ, P], F32)
    uns = sb("uns", [P, 1], F32)
    last_i = sb("last_i", [1, NU], I32)
    last_b = sb("last_b", [1, NU], I32)
    key = sb("key", [1, NU], F32)
    unit_no = sb("unit_no", [1, NU], F32)
    step_no = sb("step_no", [P, J], F32)
    prev_no = sb("prev_no", [P, J], F32)
    junk = sb("junk", [P, 2 * J, NU], F32)
    cnt = sb("cnt", [P, 2 * J], F32)
    flag = sb("flag", [P, 1], F32)
    keep = sb("keep", [P, 1], F32)
    lin = sb("lin", [P, J], F32)
    stair_b = sb("stair_b", [P, 2 * J], F32)
    diff = sb("diff", [P, J], F32)
    first = sb("first", [P, J], F32)
    fresh_f = sb("fresh_f", [P, J], F32)
    unit_f = sb("unit_f", [P, J], F32)
    win_f = sb("win_f", [P, J], F32)
    base_f = sb("base_f", [P, J], F32)
    unit_i = sb("unit_i", [P, J], I32)
    win_i = sb("win_i", [P, J], I32)
    zero_row = sb("zero_row", [1, TABW], F32)
    src_s = sb("src_s", [P, J, UE], I32)
    dst_s = sb("dst_s", [P, J, UE], I32)
    src_sf = sb("src_sf", [P, J, UE], F32)
    xs, src_t = g["xs"], g["src_t"]
    NFULL = N // P
    LISTS = 16 * 13

    with nc.Block() as block:
        @block.sync
        def _(sp):
            sp.wait_ge(pads, 4)
            for t, a, o in ((dst_d, g["dst"], 0), (nxt_d, g["dst"], 1), (src_d, g["src"], 0)):
                sp.dma_start(t[:, 0:TJ - 1, :], a[o:EFULL + o].rearrange("(j c p) -> c j p", c=P, p=P)
                             ).then_inc(lists_in, 16)
                m = EFULL + ETILES * P
                sp.dma_start(t[0:ETILES, TJ - 1, :], a[EFULL + o:m + o].rearrange("(c p) -> c p", p=P)
                             ).then_inc(lists_in, 16)
                sp.dma_start(t[ETILES:ETILES + 1, TJ - 1, 0:EREST - o],
                             a[m + o:E].rearrange("(c p) -> c p", c=1)).then_inc(lists_in, 16)
            sp.dma_start(last_i[0:1, 0:NU - 1],
                         g["dst"][0:(NU - 1) * UE].rearrange("(a u q) -> a u q", q=UE, a=1)[:, :, UE - 1],
                         allow_slow_non_contiguous=True).then_inc(lists_in, 16)
            sp.dma_start(last_i[0:1, NU - 1:NU], g["dst"][E - 1:E].rearrange("(a u) -> a u", a=1)
                         ).then_inc(lists_in, 16)
            sp.dma_start(xs[:, 0:NFULL, :], g["x"][0:NFULL * P, :].rearrange("(t p) d -> p t d", p=P)
                         ).then_inc(lists_in, 16)
            sp.dma_start(xs[0:N - NFULL * P, NFULL, :], g["x"][NFULL * P:N, :]).then_inc(lists_in, 16)
            sp.wait_ge(lists_in, LISTS)
            for r, t in enumerate((src_d, dst_d)):
                sp.dma_start(g["edges_d"][r].rearrange("u (k p) -> (u k) p", k=K).rearrange("(j c) p -> c j p", c=P),
                             t[:, :, :]).then_inc(rows_out, 16)
            sp.wait_ge(tabs_ready, 2)
            sp.dma_start(g["tabs_d"].rearrange("(j p) -> p j", p=P), win_i[:, :],
                         allow_slow_non_contiguous=True).then_inc(tabs_out, 16)
            sp.dma_start(g["fresh_d"].rearrange("(j p) -> p j", p=P), fresh_f[:, :],
                         allow_slow_non_contiguous=True).then_inc(tabs_out, 16)
            sp.wait_ge(tabs_out, 32)
            sp.dma_start(g["tab_b0"][:, :], g["tabs_d"].rearrange("(a s) -> a s", a=1)).then_inc(tabs_in, 16)
            sp.dma_start(g["fresh"][:, :], g["fresh_d"].partition_broadcast(HW)).then_inc(tabs_in, 16)
            sp.wait_ge(tabs_in, 32)

        @block.gpsimd
        def _(pool):
            pool.memset(dst_d[:, TJ - 1, :], -1).then_inc(pads, 1)
            pool.memset(nxt_d[:, TJ - 1, :], 1 << 20).then_inc(pads, 1)
            pool.memset(src_d[:, TJ - 1, :], 0).then_inc(pads, 1)
            pool.memset(xs[:, NFULL, :], 0.0).then_inc(pads, 1)
            pool.memset(g["ident"][:, :], 0.0).then_inc(id_zero, 1)
            pool.memset(g["ones"][:, :], 1.0).then_inc(consts, 1)
            pool.memset(g["eps_t"][:, :], EPS).then_inc(consts, 1)
            pool.memset(zero_row[:, :], 0.0).then_inc(consts, 1)
            pool.wait_ge(id_zero, 1)
            pool.affine_select(out=g["ident"][:, :], in_=g["ident"][:, :], compare_op=ALU.not_equal, fill=1.0,
                               base=0, pattern=[[-1, P]], channel_multiplier=1).then_inc(consts, 1)
            pool.memset(g["mask_sel"][:, :], 0.0).then_inc(id_zero, 1)
            pool.wait_ge(id_zero, 2)
            pool.affine_select(out=g["mask_sel"][0:W, :], in_=g["mask_sel"][0:W, :], compare_op=ALU.not_equal,
                               fill=MASK, base=0, pattern=[[0, H], [-1, W]], channel_multiplier=1
                               ).then_inc(consts, 1)
            for q in range(3):
                pool.wait_ge(consts, 5 + q)
                pool.iota(g["win_col"][W * q:W * q + W, :], [[0, 1]], base=0, channel_multiplier=1,
                          allow_small_or_imprecise_dtypes=True).then_inc(consts, 1)
            pool.wait_ge(consts, 8)
            pool.iota(unit_no[:, :], [[1, NU]], base=0, channel_multiplier=0,
                      allow_small_or_imprecise_dtypes=True).then_inc(consts, 1)
            pool.iota(step_no[:, :], [[P, J]], base=0, channel_multiplier=1,
                      allow_small_or_imprecise_dtypes=True).then_inc(consts, 1)
            pool.wait_ge(rows_out, 32)
            pool.wait_ge(units_ready, 1)
            for r, t in enumerate((src_s, dst_s)):
                for j in range(J):
                    pool.indirect_dma_start(t[:, j, :], None, g["edges_d"][r],
                                            bass.IndirectOffsetOnAxis(ap=unit_i[:, j:j + 1], axis=0)
                                            ).then_inc(steps_in, 16)
            pool.wait_ge(steps_in, 16 * 2 * J)

        @block.vector
        def _(v):
            n = [0]

            def link(ins):
                n[0] += 1
                ins.then_inc(chain, 1)
                v.wait_ge(chain, n[0])

            v.wait_ge(lists_in, LISTS)
            v.wait_ge(consts, 10)
            v.tensor_copy(dst_f[:, :, :], dst_d[:, :, :]).then_inc(src_cast, 1)
            link(v.tensor_copy(nxt_f[:, :, :], nxt_d[:, :, :]))
            link(v.tensor_tensor(nxt_f[:, :, :], dst_f[:, :, :], nxt_f[:, :, :], ALU.is_gt))
            v.tensor_reduce(uns[:, :], nxt_f[:, :, :].rearrange("p j c -> p (j c)"), AX, ALU.max).then_inc(marks, 1)
            link(v.tensor_scalar(last_b[:, :], last_i[:, :], W.bit_length() - 1, None, ALU.arith_shift_right))
            link(v.tensor_copy(key[:, :], last_b[:, :]))
            link(v.tensor_tensor(key[:, :], key[:, :], unit_no[:, :], ALU.add))
            v.memset(key[0:1, NU - 1:NU], float(NU + NB - 2)).then_inc(marks, 1)
            link(v.tensor_scalar(prev_no[:, :], step_no[:, :], -1.0, None, ALU.add))
            v.wait_ge(spread, 1)
            link(v.tensor_scalar(flag[:, :], ps[1][:, 0:1], 1.0, None, ALU.min))
            link(v.tensor_scalar(keep[:, :], flag[:, :], -1.0, 1.0, ALU.mult, ALU.add))
            for j in range(2 * J):
                no = step_no if j < J else prev_no
                link(v.tensor_scalar(junk[:, j, :], ps[0][:, 0:NU], no[:, j % J:j % J + 1], 0.0, ALU.is_lt, ALU.add,
                                     accum_out=cnt[:, j:j + 1]))
            link(v.tensor_tensor(stair_b[:, 0:J], step_no[:, :], cnt[:, 0:J], ALU.subtract))
            link(v.tensor_tensor(stair_b[:, J:2 * J], prev_no[:, :], cnt[:, J:2 * J], ALU.subtract))
            link(v.tensor_scalar(stair_b[:, :], stair_b[:, :], float(NB - 1), None, ALU.min))
            link(v.tensor_scalar(lin[:, :], step_no[:, :], float(NU), flag[:, 0:1], ALU.min, ALU.mult))
            link(v.scalar_tensor_tensor(unit_f[:, :], cnt[:, 0:J], keep[:, 0:1], lin[:, :], ALU.mult, ALU.add))
            v.tensor_copy(unit_i[:, :], unit_f[:, :]).then_inc(units_ready, 1)
            link(v.tensor_scalar(win_f[:, :], stair_b[:, 0:J], keep[:, 0:1], None, ALU.mult))
            v.tensor_copy(win_i[:, :], win_f[:, :]).then_inc(tabs_ready, 1)
            link(v.tensor_tensor(diff[:, :], stair_b[:, 0:J], stair_b[:, J:2 * J], ALU.is_gt))
            link(v.tensor_scalar(first[:, :], step_no[:, :], 0.0, keep[:, 0:1], ALU.is_equal, ALU.max))
            link(v.tensor_tensor(diff[:, :], diff[:, :], first[:, :], ALU.mult))
            v.tensor_scalar(fresh_f[:, :], diff[:, :], FRESH, None, ALU.mult).then_inc(tabs_ready, 1)
            link(v.tensor_scalar(base_f[:, :], win_f[:, :], float(W), None, ALU.mult))
            link(v.tensor_scalar(g["next_w"][:, :], flag[:, :], -float(W), None, ALU.mult))
            link(v.tensor_scalar(g["back_w"][:, :], flag[:, :], float(NB * W), None, ALU.mult))
            link(v.tensor_scalar(g["flag_row"][:, :], zero_row[:, :], flag[0:1, 0:1], None, ALU.add))
            link(v.tensor_scalar(g["n_pass_t"][:, :], flag[0:1, 0:1], float(NB - 1), 1.0, ALU.mult, ALU.add))
            v.wait_ge(steps_in, 16 * 2 * J)
            v.tensor_copy(src_sf[:, :, :], src_s[:, :, :]).then_inc(src_cast, 1)
            for j in range(J):
                v.tensor_scalar(g["rel_s"][:, j, :], dst_s[:, j, :], base_f[:, j:j + 1], g["next_w"][:, 0:1],
                                ALU.subtract, ALU.subtract).then_inc(chain, 1)
            for j in range(J):
                for t in range(K):
                    c = j * K + t
                    v.wait_ge(turned, c + 1)
                    v.tensor_copy(src_t[:, P * j:P * j + P, t], ps[2 + c % 2][:, 0:P]).then_inc(copied, 1)

        @block.tensor
        def _(pe):
            pe.wait_ge(consts, 10)
            pe.wait_ge(marks, 2)
            pe.matmul(ps[0][:, 0:NU], g["ones"][0:1, :], key[:, :], start=True, stop=True)
            pe.matmul(ps[1][:, 0:1], g["ones"][:, :], uns[:, :], start=True, stop=True).then_inc(spread, 1)
            pe.wait_ge(src_cast, 2)
            for c in range(J * K):
                if c >= 2:
                    pe.wait_ge(copied, c - 1)
                pe.transpose(ps[2 + c % 2][:, 0:P], src_sf[:, c // K, c % K * P:c % K * P + P], g["ident"][:, :]
                             ).then_inc(turned, 1)


def hold(eng, semaphore, value, gate=None):
    if isinstance(value, int) and value <= 0:
        return
    eng.wait_ge(semaphore, value)
    if gate is not None:
        eng.sem_inc(gate)


def turns(eng, body):
    body(0)
    with eng.Fori(1, NT // UT) as g:
        body(g)


def row_bc(ap, n):
    return ap.unsqueeze(2).to_broadcast([ap.shape[0], ap.shape[1], n])


def center(v, link, src3, dst3, sq3, mean):
    link(v.tensor_reduce(mean[:, :], src3[:, :, :], AX, ALU.add))
    link(v.tensor_scalar(mean[:, :], mean[:, :], 1.0 / D, None, ALU.mult))
    link(v.tensor_tensor(dst3[:, :, :], src3[:, :, :], row_bc(mean[:, :], D), ALU.subtract))


def load_weights(sp, w, layer, done):
    l1 = bass.ds(layer, 1)
    loads = [
        (w["wlr"][:, 0:HD], w["Wl"][l1].rearrange("l d f -> (l d) f")),
        (w["wlr"][:, HD:2 * HD], w["Wr"][l1].rearrange("l d f -> (l d) f")),
        (w["blr"][:, 0:HD], w["bl"][l1].rearrange("l f -> (l f)").partition_broadcast(P)),
        (w["blr"][:, HD:2 * HD], w["br"][l1].rearrange("l f -> (l f)").partition_broadcast(P)),
        (w["att_row"][:, :], w["att"][l1].rearrange("l h f -> (l h f)").partition_broadcast(P)),
        (w["pb_row"][:, :], w["proj_b"][l1].rearrange("l f -> (l f)").partition_broadcast(P)),
        (w["b2_row"][:, :], w["b2"][l1].rearrange("l f -> (l f)").partition_broadcast(P)),
        (w["w1"][:, :], w["W1"][l1].rearrange("l d f -> (l d) f")),
        (w["pw"][:, :, :], w["proj_W"][l1].rearrange("l (h f) d -> f (l h) d", h=H)),
        (w["w2"][:, :, :], w["W2"][l1].rearrange("l (c f) d -> f (l c) d", f=P)),
        (w["gat_col"][:, :], w["gat_b"][l1].rearrange("l (h f) -> f (l h)", h=H)),
        (w["b1_col"][:, :], w["b1"][l1].rearrange("l (c f) -> f (l c)", f=P)),
    ] + [(w["gcol"][:, i:i + 1], w[k][l1].rearrange("l f -> f l"))
         for i, k in enumerate(("ln1_g", "ln1_b", "ln2_g", "ln2_b"))]
    for to, of in loads:
        sp.dma_start(to, of, allow_slow_non_contiguous=True).then_inc(done, 16)
    return 16 * len(loads)


def project_nodes(nc, sb, sem, ps, w, s, layer):
    weights_in = sem("weights_in")
    chain = sem("chain")
    centered = sem("centered")
    squared = sem("squared")
    var_ready = sem("var_ready")
    std_ready = sem("std_ready")
    xn_ready = sem("xn_ready")
    xn_turned = sem("xn_turned")
    h_ready = sem("h_ready")
    proj_ready = sem("proj_ready")
    proj_read = sem("proj_read")
    xr_ready = sem("xr_ready")
    hi_ready = sem("hi_ready")
    rest_ready = sem("rest_ready")
    mid_ready = sem("mid_ready")
    row_ready = sem("row_ready")
    split_ready = sem("split_ready")
    row_out = [sem(f"row_out{i}") for i in range(UT)]
    split_out = [sem(f"split_out{i}") for i in range(UT)]
    xr3_in = sem("xr3_in")
    state = sem("state")
    link_s = sem("link_s")
    var = sb("var", [P, NT], F32)
    sq = sb("sq", [P, NT, P], F32)
    xn = sb("xn", [P, UT, P], F32)
    hT = sb("hT", [P, UT, P], F32)
    row = sb("row", [P, UT, H, RC], F32)
    xrf = sb("xrf", [P, UT, XC], F32)
    rest = sb("rest", [P, UT, XC], F32)
    split = sb("split", [P, UT, 3, XC], BF16)
    xc = sb("xc", [P, NT, P], F32)
    xs, mean, rstd = s["xs"], s["mean"], s["rstd"]
    NWTS = 16 * 16
    bank_t = [0, 1, 2, 0, 1]
    bank_p = [3, 4, 5, 3, 4]

    with nc.Block() as block:
        @block.sync
        def _(sp):
            assert load_weights(sp, w, layer, weights_in) == NWTS
            @partial(turns, sp)
            def _(g):
                for k in range(UT):
                    i = g * UT + k
                    hold(sp, row_ready, i + 1, link_s)
                    sp.dma_start(s["table"][bass.ds(i * P, P), :], row[:, k, :, :].rearrange("p h c -> p (h c)")
                                 ).then_inc(row_out[k], 16)
                    hold(sp, split_ready, i + 1, link_s)
                    sp.dma_start(s["xr_split"][:, bass.ds(i * P, P), :].rearrange("q n c -> n q c"),
                                 split[:, k, :, :]).then_inc(split_out[k], 16)
            for k in range(UT):
                sp.wait_ge(row_out[k], 16 * (NT // UT))
                sp.wait_ge(split_out[k], 16 * (NT // UT))
            for q in range(3):
                sp.dma_start(s["xr3"][W * q:W * q + W, :, :],
                             s["xr_split"][q, 0:NB * W, :].rearrange("(b j) c -> j b c", j=W)).then_inc(xr3_in, 16)
            sp.wait_ge(xr3_in, 48)
            sp.wait_ge(weights_in, NWTS)

        @block.gpsimd
        def _(pool):
            pool.memset(s["acc"][:, :, :], 0.0).then_inc(state, 1)
            pool.memset(row[:, :, :, D:D + 1], 1.0).then_inc(state, 1)
            pool.tensor_copy(s["tab_b"][:, :], s["tab_b0"][:, :]).then_inc(state, 1)

        @block.vector
        def _(v):
            n = [0]

            def link(ins):
                n[0] += 1
                ins.then_inc(chain, 1)
                v.wait_ge(chain, n[0])

            center(v, link, xs, xc, sq, mean)
            v.tensor_copy(mean[:, 0:1], mean[:, 0:1]).then_inc(centered, 1)
            v.wait_ge(squared, 1)
            v.tensor_reduce(var[:, :], sq[:, :, :], AX, ALU.add).then_inc(var_ready, 1)
            v.wait_ge(std_ready, 1)
            link(v.reciprocal(rstd[:, :], rstd[:, :]))
            v.wait_ge(weights_in, NWTS)
            v.wait_ge(state, 3)
            link(v.tensor_scalar(s["att08"][:, :], w["att_row"][:, :], 1.0 - SLOPE, None, ALU.mult))
            base = n[0]
            @partial(turns, v)
            def _(g):
                for k in range(UT):
                    i = g * UT + k
                    v.tensor_scalar(xn[:, k, :], xc[:, bass.ds(i, 1), :].rearrange("p a d -> p (a d)"),
                                    rstd[:, bass.ds(i, 1)], None, ALU.mult).then_inc(xn_ready, 1)
                for k in range(UT):
                    i = g * UT + k
                    hold(v, proj_ready, i + 1)
                    pp = ps[bank_p[k]]
                    hold(v, row_out[k], g * 16)
                    v.tensor_tensor(row[:, k, :, 0:D], pp[:, 0:HD].rearrange("p (h d) -> p h d", h=H),
                                    w["blr"][:, 0:HD].rearrange("p (h d) -> p h d", h=H), ALU.add
                                    ).then_inc(proj_read, 1)
                    hold(v, mid_ready, g * UT)
                    v.tensor_tensor(xrf[:, k, 0:HD], pp[:, HD:2 * HD], w["blr"][:, HD:2 * HD], ALU.add
                                    ).then_inc(proj_read, 1)
                    hold(v, proj_read, 2 * i + 2)
                    for h in range(H):
                        a = w["att_row"][:, h * D:h * D + D]
                        r1 = v.tensor_tensor_reduce(sq[:, 2 * H * k + h, :], row[:, k, h, 0:D], a, SLOPE / D, 0.0, ALU.mult, ALU.add,
                                                    row[:, k, h, D + 1:D + 2])
                        r1.then_inc(row_ready, 1) if h == H - 1 else r1.then_inc(link_s, 1)
                        r2 = v.tensor_tensor_reduce(sq[:, 2 * H * k + H + h, :], xrf[:, k, h * D:h * D + D], a, SLOPE, 0.0, ALU.mult,
                                                    ALU.add, xrf[:, k, HD + h:HD + h + 1])
                        r2.then_inc(xr_ready, 1)
                for k in range(UT):
                    i = g * UT + k
                    hold(v, hi_ready, i + 1)
                    v.tensor_tensor(rest[:, k, :], xrf[:, k, :], split[:, k, 0, :], ALU.subtract
                                    ).then_inc(rest_ready, 1)
                for k in range(UT):
                    i = g * UT + k
                    hold(v, mid_ready, i + 1)
                    v.tensor_tensor(split[:, k, 2, :], rest[:, k, :], split[:, k, 1, :], ALU.subtract
                                    ).then_inc(split_ready, 1)

        @block.scalar
        def _(act):
            act.wait_ge(centered, 1)
            act.activation(sq[:, :, :], xc[:, :, :], ACT.Square).then_inc(squared, 1)
            act.wait_ge(var_ready, 1)
            act.activation(rstd[:, :], var[:, :], ACT.Sqrt, bias=s["eps_t"][:, 0:1], scale=1.0 / D
                           ).then_inc(std_ready, 1)
            act.wait_ge(weights_in, NWTS)
            @partial(turns, act)
            def _(g):
                for k in range(UT):
                    i = g * UT + k
                    hold(act, xn_turned, i + 1)
                    hold(act, proj_ready, g * UT) if k == 0 else None
                    act.activation(hT[:, k, :], ps[bank_t[k]][:, 0:P], ACT.Identity, bias=w["gcol"][:, 1:2],
                                   scale=w["gcol"][:, 0:1]).then_inc(h_ready, 1)
                for k in range(UT):
                    i = g * UT + k
                    hold(act, xr_ready, 2 * i + 2)
                    hold(act, split_out[k], g * 16)
                    act.copy(split[:, k, 0, :], xrf[:, k, :]).then_inc(hi_ready, 1)
                for k in range(UT):
                    i = g * UT + k
                    hold(act, rest_ready, i + 1)
                    act.copy(split[:, k, 1, :], rest[:, k, :]).then_inc(mid_ready, 1)

        @block.tensor
        def _(pe):
            pe.wait_ge(weights_in, NWTS)
            @partial(turns, pe)
            def _(g):
                for k in range(UT + 1):
                    if k < UT:
                        i = g * UT + k
                        hold(pe, xn_ready, i + 1)
                        if k in (0, 1, 3, 4):
                            hold(pe, h_ready, (g * UT + k - 1) if k else g * UT)
                        pe.transpose(ps[bank_t[k]][:, 0:P], xn[:, k, :], s["ident"][:, :]).then_inc(xn_turned, 1)
                    if k:
                        j = k - 1
                        i = g * UT + j
                        hold(pe, h_ready, i + 1)
                        hold(pe, proj_read, 2 * i if j == 0 else 2 * (i - 1))
                        pe.matmul(ps[bank_p[j]][:, :], hT[:, j, :], w["wlr"][:, :], start=True, stop=True
                                  ).then_inc(proj_ready, 1)


def lay_out_steps(nc, sb, sem, ps, s):
    rel_ready = sem("rel_ready")
    stored = sem("stored")
    rel_h = sb("rel_h", [P, TABW // P, UE], I16)
    with nc.Block() as block:
        @block.vector
        def _(v):
            v.tensor_scalar(s["rel_s"][:, :, :], s["rel_s"][:, :, :], s["next_w"][:, 0:1], None, ALU.add
                            ).then_inc(rel_ready, 1)
            v.wait_ge(rel_ready, 1)
            v.tensor_copy(rel_h[:, :, :], s["rel_s"][:, :, :]).then_inc(rel_ready, 1)

        @block.sync
        def _(sp):
            sp.wait_ge(rel_ready, 2)
            sp.dma_start(s["rel_d"].rearrange("(j p e) -> p j e", p=P, e=UE), rel_h[:, :, :]).then_inc(stored, 16)
            sp.wait_ge(stored, 16)


def edge_pass(nc, sb, sem, ps, s):
    rows_in = [sem(f"rows_in{i}") for i in range(RING)]
    idx_ready = sem("idx_ready")
    rel_in = [sem(f"rel_in{i}") for i in range(2)]
    one_hot_ready = sem("one_hot_ready")
    z_ready = sem("z_ready")
    prods_ready = sem("prods_ready")
    dots_done = sem("dots_done")
    score_ready = sem("score_ready")
    masked = sem("masked")
    top_ready = sem("top_ready")
    top_turned = sem("top_turned")
    unit_max = sem("unit_max")
    new_max = sem("new_max")
    drop_ready = sem("drop_ready")
    max_spread = sem("max_spread")
    shifted = sem("shifted")
    weights_ready = sem("weights_ready")
    sums_ready = sem("sums_ready")
    merged = sem("merged")
    kept = sem("kept")
    begun = sem("begun")
    gate = sem("gate")
    tab_next = sem("tab_next")

    rows = sb("rows", [P, RING, K, H, RC], F32)
    idx = sb("idx", [P, 2, RING, K], I32)
    relb = sb("relb", [3 * W, 2, RING, UE], I16)
    oh = sb("oh", [3 * W, 2, UE], BF16)
    prods = sb("prods", [P, 2, K * H, D], F32)
    dots = sb("dots", [P, 2, K * H], F32)
    score = sb("score", [P, 2, K * H], F32)
    msc = sb("msc", [P, 4, K * H, W], F32)
    top = sb("top", [P, 2, HW], F32)
    umax = sb("umax", [HW, 1], F32)
    nmax = sb("nmax", [HW, 2, 1], F32)
    drop = sb("drop", [HW, 4, 1], F32)
    dmax = sb("dmax", [P, 2, K * HW], F32)
    wgt = sb("wgt", [P, 2, K, HW], F32)
    decay = sb("decay", [HW, 4, 1], F32)
    carry = sb("carry", [HW, 2, D + 1], F32)
    BZ, BR, BT, BS = (0, 1), (2, 3, 4), 5, (6, 7)
    TM = P
    MS = 8
    acc = s["acc"]

    def exists(i, lag):
        return not isinstance(i, int) or 0 <= i - lag < NS

    def groups(eng, tick, lo, tail):
        for k in range(RING):
            tick(k, lambda c, k=k: k + c, 0)
        with eng.Fori(1, GROUPS) as g:
            r = {c: eng.snap(g * RING + c) for c in range(lo, RING + 2)}
            for k in range(RING):
                tick(k, lambda c, k=k: r[k + c], g)
        for k in range(tail):
            tick(k, lambda c, k=k: NS + k + c, GROUPS)

    def pairs(eng, tick, lo, tail):
        for k in range(RING):
            tick(k, lambda c, k=k: k + c, 0, 0)
        with eng.Fori(1, HALVES) as h:
            for half in (1, 0):
                r = {c: eng.snap(h * (2 * RING) - half * RING + c) for c in range(lo, RING + 2)}
                for k in range(RING):
                    tick(k, lambda c, k=k: r[k + c], half, h)
        for k in range(tail):
            tick(k, lambda c, k=k: NS + k + c, 0, HALVES)

    with nc.Block() as block:
        @block.gpsimd
        def _(pool):
            def take(half, first):
                pool.tensor_copy(idx[:, half, :, :], s["src_t"][:, bass.ds(first, RING), :]).then_inc(idx_ready, 1)

            def tick(k, at, half, turn):
                i = at(0)
                hold(pool, sums_ready, at(1 - RING), gate)
                if k == 0:
                    hold(pool, idx_ready, turn * 2 - half + 1, gate)
                for t in range(K):
                    pool.indirect_dma_start(rows[:, k, t, :, :].rearrange("p h c -> p (h c)"), None,
                                            s["table"][:, :],
                                            bass.IndirectOffsetOnAxis(ap=idx[:, half, k, t:t + 1], axis=0)
                                            ).then_inc(rows_in[k], 16)
                if k == RING - 1:
                    take(1 - half, at(1))

            take(0, 0)
            pairs(pool, tick, 1 - RING, 0)
            for k in range(RING):
                pool.wait_ge(rows_in[k], 16 * K * GROUPS)
            pool.wait_ge(idx_ready, GROUPS + 1)

        @block.sync
        def _(sp):
            def load(half, first):
                sp.dma_start(relb[:, half, :, :].rearrange("p k e -> p (k e)"),
                             s["rel_d"][bass.ds(first, RING * UE)].partition_broadcast(3 * W)
                             ).then_inc(rel_in[half], 16)
            load(0, 0)
            load(1, RING * UE)
            with sp.Fori(1, HALVES) as h:
                for half in range(2):
                    sp.wait_ge(one_hot_ready, h * 2 * RING + (half - 1) * RING)
                    sp.sem_inc(gate)
                    load(half, (h * 2 + half) * (RING * UE))
            for half in range(2):
                sp.wait_ge(rel_in[half], 16 * HALVES)


        @block.tensor
        def _(pe):
            def tick(k, at, turn):
                i = at(0)
                if exists(i, 0):
                    b = pe.value_load(s["tab_b"][0:1, bass.ds(i, 1)], min_val=0, max_val=NB - 1)
                    hold(pe, one_hot_ready, at(1), gate)
                elif exists(i, 3):
                    hold(pe, top_ready, at(-2), gate)
                elif exists(i, 4):
                    hold(pe, new_max, at(-3), gate)
                if exists(i, 3):
                    pe.transpose(ps[BT][0:HW, 0:P], top[:, (k - 3) % 2, :], s["ident"][:, :]
                                 ).then_inc(top_turned, 1)
                if exists(i, 4):
                    pe.transpose(ps[BT][:, TM:TM + HW], nmax[:, k % 2, :].to_broadcast([HW, P]),
                                 s["ident"][0:HW, 0:HW]).then_inc(max_spread, 1)
                if exists(i, 0):
                    z, lin = ps[BZ[k % 2]], ps[BR[k % 3]]
                    pe.wait_ge(rows_in[k], turn * (16 * K) + 16 * K)
                    pe.sem_inc(gate)
                    for t in range(K):
                        pe.matmul(z[:, t * HD:t * HD + HD], s["ident"][:, :], rows[:, k, t, :, 0:D],
                                  start=(t == 0), stop=False)
                    xr_b = s["xr3"][:, bass.ds(b, 1), :].rearrange("p a c -> p (a c)")
                    for t in range(K):
                        sel = oh[:, k % 2, t * P:t * P + P]
                        pe.matmul(lin[:, MS + t * HW:MS + t * HW + HW], sel, s["mask_sel"][:, :], start=(t == 0),
                                  stop=False)
                        pe.matmul(lin[:, t * H:t * H + H], sel, xr_b[:, HD:XC], start=False, stop=(t == K - 1))
                        m = pe.matmul(z[:, t * HD:t * HD + HD], sel, xr_b[:, 0:HD], start=False,
                                      stop=(t == K - 1))
                    m.then_inc(z_ready, 1)
                if exists(i, 5):
                    hold(pe, weights_ready, at(-4))
                    if not exists(i, 0):
                        hold(pe, merged, at(-6))
                    kk = (k - 5) % RING
                    out = ps[BS[kk % 2]]
                    for t in range(K):
                        for h in range(H):
                            m = pe.matmul(out[h * W:h * W + W, 0:D + 1], wgt[:, kk % 2, t, h * W:h * W + W],
                                          rows[:, kk, t, h, 0:D + 1], start=(t == 0), stop=(t == K - 1))
                    m.then_inc(sums_ready, 1)
            groups(pe, tick, -6, 5)

        @block.scalar
        def _(act):
            def tick(k, at, turn):
                i = at(0)
                if exists(i, 7):
                    b = act.value_load(s["tab_b"][0:1, bass.ds(at(-7), 1)], min_val=0, max_val=NB - 1)
                    hold(act, merged, at(-6))
                    hold(act, kept, at(-7))
                    act.copy(acc[:, bass.ds(b, 1), :].rearrange("p a c -> p (a c)"), carry[:, (k - 7) % 2, :]
                             ).then_inc(kept, 1)
                if exists(i, 1):
                    p, kk = (k - 1) % 2, (k - 1) % RING
                    hold(act, prods_ready, at(0))
                    for t in range(K):
                        for h in range(H):
                            c = t * H + h
                            m = act.activation(prods[:, p, c, :], prods[:, p, c, :], ACT.Identity,
                                               bias=rows[:, kk, t, h, D + 1:D + 2], accum_out=dots[:, p, c:c + 1])
                    m.then_inc(dots_done, 1)
                if exists(i, 4):
                    p = k % 2
                    hold(act, shifted, at(-3))
                    act.activation(decay[:, k % 4, :], drop[:, k % 4, :], ACT.Exp)
                    act.activation(wgt[:, p, :, :].rearrange("p t c -> p (t c)"), dmax[:, p, :], ACT.Exp
                                   ).then_inc(weights_ready, 1)
            groups(act, tick, -7, 7)

        @block.vector
        def _(v):
            def one_hot(k, at, c, half):
                kk = (k + c) % RING
                v.tensor_scalar(oh[:, kk % 2, :], relb[:, half if k + c < RING else 1 - half, kk, :],
                                s["win_col"][:, 0:1], None, ALU.is_equal).then_inc(one_hot_ready, 1)

            def tick(k, at, half, turn):
                i = at(0)
                p = k % 2
                if exists(i, 1):
                    q = (k - 1) % 2
                    hold(v, z_ready, at(0))
                    v.scalar_tensor_tensor(prods[:, q, :, :].rearrange("p (t h) d -> p t (h d)", t=K),
                                           ps[BZ[q]][:, :].rearrange("p (t c) -> p t c", t=K), 0.0,
                                           s["att08"][:, :].unsqueeze(1).to_broadcast([P, K, HD]),
                                           ALU.max, ALU.mult).then_inc(prods_ready, 1)
                if exists(i, 3):
                    hold(v, max_spread if exists(i, 4) else top_turned, at(-3) if exists(i, 4) else at(-2))
                    v.tensor_reduce(umax[:, :], ps[BT][0:HW, 0:P], AX, ALU.max).then_inc(unit_max, 1)
                if exists(i, 2):
                    hold(v, dots_done, at(-1))
                    v.tensor_tensor(score[:, p, :], dots[:, p, :], ps[BR[(k - 2) % 3]][:, 0:K * H], ALU.add
                                    ).then_inc(score_ready, 1)
                if exists(i, 4):
                    if not exists(i, 3):
                        hold(v, max_spread, at(-3))
                    if not exists(i, 2):
                        hold(v, weights_ready, at(-5))
                    v.tensor_tensor(dmax[:, p, :].rearrange("p (t c) -> p t c", t=K),
                                    msc[:, k % 4, :, :].rearrange("p (t h) w -> p t (h w)", t=K),
                                    ps[BT][:, TM:TM + HW].unsqueeze(1).to_broadcast([P, K, HW]), ALU.subtract
                                    ).then_inc(shifted, 1)
                if exists(i, 3):
                    q = (k - 3) % 2
                    fresh = s["fresh"][:, bass.ds(at(-3), 1)]
                    hold(v, unit_max, at(-2))
                    v.scalar_tensor_tensor(nmax[:, q, :], nmax[:, 1 - q, :], fresh, umax[:, :], ALU.add, ALU.max
                                           ).then_inc(new_max, 1)
                if exists(i, 2):
                    hold(v, score_ready, at(-1))
                    v.scalar_tensor_tensor(msc[:, (k - 2) % 4, :, :],
                                           ps[BR[(k - 2) % 3]][:, MS:MS + K * HW].rearrange("p (c w) -> p c w", w=W),
                                           -MASK, score[:, p, :].unsqueeze(2).to_broadcast([P, K * H, W]),
                                           ALU.add, ALU.add).then_inc(masked, 1)
                if exists(i, 3):
                    hold(v, new_max, at(-2))
                    v.scalar_tensor_tensor(drop[:, (k - 3) % 4, :], nmax[:, 1 - q, :], fresh, nmax[:, q, :],
                                           ALU.add, ALU.subtract).then_inc(drop_ready, 1)
                if exists(i, 6):
                    hold(v, sums_ready, at(-5))
                    hold(v, merged, at(-6))
                    if not exists(i, 2):
                        hold(v, kept, at(-7))
                    v.scalar_tensor_tensor(carry[:, p, :], carry[:, 1 - p, :], decay[:, (k - 6) % 4, :],
                                           ps[BS[p]][0:HW, 0:D + 1], ALU.mult, ALU.add).then_inc(merged, 1)
                if exists(i, 2):
                    hold(v, masked, at(-1))
                    m4 = msc[:, (k - 2) % 4, :, :].rearrange("p (t h) w -> p t (h w)", t=K)
                    v.scalar_tensor_tensor(top[:, p, :], m4[:, 0, :], FLOOR, m4[:, 1, :], ALU.max, ALU.max
                                           ).then_inc(top_ready, 1)
                if k == RING - 1 and exists(i, -1):
                    v.wait_ge(rel_in[1 - half], turn * 16 + 16)
                if exists(i, -1):
                    one_hot(k, at, 1, half)

            v.memset(nmax[:, 1, :], 0.0).then_inc(begun, 1)
            v.memset(carry[:, 1, :], 0.0).then_inc(begun, 1)
            v.wait_ge(begun, 2)
            v.wait_ge(rel_in[0], 16)
            one_hot(0, lambda c: c, 0, 0)
            pairs(v, tick, -7, 6)
            v.wait_ge(kept, NS)
            v.tensor_tensor(s["tab_b"][:, :], s["tab_b"][:, :], s["flag_row"][:, :], ALU.add).then_inc(tab_next, 1)


def update_nodes(nc, sb, sem, ps, w, s):
    chain = sem("chain")
    att_ready = sem("att_ready")
    att_turned = sem("att_turned")
    gt_ready = sem("gt_ready")
    proj_ready = sem("proj_ready")
    x_ready = sem("x_ready")
    centered = sem("centered")
    squared = sem("squared")
    var_ready = sem("var_ready")
    std_ready = sem("std_ready")
    xn_ready = sem("xn_ready")
    xn_turned = sem("xn_turned")
    h_ready = sem("h_ready")
    up_ready = sem("up_ready")
    gelu_ready = sem("gelu_ready")
    down_ready = sem("down_ready")
    y_ready = sem("y_ready")
    link_s = sem("link_s")
    rel_back = sem("rel_back")
    q = P // W
    gT = sb("gT", [P, UT, H, P], F32)
    rden = sb("rden", [HW, NBP], F32)
    sq = sb("sq", [P, NT, P], F32)
    var = sb("var", [P, NT], F32)
    xn = sb("xn", [P, UT, P], F32)
    hT = sb("hT", [P, UT, P], F32)
    ge = sb("ge", [P, UT, MLP // P, P], F32)
    an = ge[0:HW, :, 0:q, :]
    tmp = sb("tmp", [P, UT, P], F32)
    xc = sb("xc", [P, NT, P], F32)
    xs, mean, rstd, acc = s["xs"], s["mean"], s["rstd"], s["acc"]
    bank = [0, 1, 2, 0, 1]
    bank2 = [3, 4, 5, 3, 4]
    bank3 = [6, 7, 6, 7, 6]

    def tile(ap, i):
        return ap[:, bass.ds(i, 1), :].rearrange("p a d -> p (a d)")

    with nc.Block() as block:
        @block.vector
        def _(v):
            n = [0]

            def link(ins):
                n[0] += 1
                ins.then_inc(chain, 1)
                v.wait_ge(chain, n[0])

            v.tensor_scalar(s["rel_s"][:, :, :], s["rel_s"][:, :, :], s["back_w"][:, 0:1], None, ALU.add
                            ).then_inc(rel_back, 1)
            link(v.tensor_scalar(rden[:, :], acc[:, :, D], 1e-16, None, ALU.add))
            link(v.reciprocal(rden[:, :], rden[:, :]))
            @partial(turns, v)
            def _(g):
                for k in range(UT):
                    i = g * UT + k
                    v.tensor_tensor(an[:, k, :, :], acc[:, bass.ds(i * q, q), 0:D],
                                    row_bc(rden[:, bass.ds(i * q, q)], D), ALU.mult).then_inc(att_ready, 1)
                for k in range(UT):
                    i = g * UT + k
                    hold(v, proj_ready, i + 1)
                    v.tensor_tensor(tmp[:, k, :], ps[bank2[k]][:, 0:P], w["pb_row"][:, :], ALU.add
                                    ).then_inc(y_ready, 1)
                    hold(v, y_ready, i + 1)
                    v.tensor_tensor(tile(xs, i), tile(xs, i), tmp[:, k, :], ALU.add).then_inc(x_ready, 1)
            v.wait_ge(x_ready, NT)
            center(v, link, xs, xc, sq, mean)
            v.tensor_copy(mean[:, 0:1], mean[:, 0:1]).then_inc(centered, 1)
            v.wait_ge(squared, 1)
            v.tensor_reduce(var[:, :], sq[:, :, :], AX, ALU.add).then_inc(var_ready, 1)
            v.wait_ge(std_ready, 1)
            link(v.reciprocal(rstd[:, :], rstd[:, :]))
            @partial(turns, v)
            def _(g):
                for k in range(UT):
                    i = g * UT + k
                    v.tensor_scalar(xn[:, k, :], tile(xc, i), rstd[:, bass.ds(i, 1)], None, ALU.mult
                                    ).then_inc(xn_ready, 1)
                for k in range(UT):
                    i = g * UT + k
                    hold(v, down_ready, i + 1)
                    v.tensor_tensor(tmp[:, k, :], ps[bank3[k]][:, 0:P], w["b2_row"][:, :], ALU.add
                                    ).then_inc(y_ready, 1)
                    hold(v, y_ready, NT + i + 1)
                    v.tensor_tensor(tile(xs, i), tile(xs, i), tmp[:, k, :], ALU.add).then_inc(x_ready, 1)

        @block.scalar
        def _(act):
            @partial(turns, act)
            def _(g):
                for k in range(UT):
                    i = g * UT + k
                    hold(act, att_turned, i + 1)
                    if k == 0:
                        hold(act, proj_ready, g * UT)
                    t4 = ps[bank[k]][:, 0:q * HW].rearrange("p (q h w) -> p q h w", q=q, h=H)
                    for h in range(H):
                        act.activation(gT[:, k, h, :].rearrange("p (q w) -> p q w", q=q), t4[:, :, h, :],
                                       ACT.Identity, bias=w["gat_col"][:, h:h + 1]).then_inc(gt_ready, 1)
            act.wait_ge(centered, 1)
            act.activation(sq[:, :, :], xc[:, :, :], ACT.Square).then_inc(squared, 1)
            act.wait_ge(var_ready, 1)
            act.activation(rstd[:, :], var[:, :], ACT.Sqrt, bias=s["eps_t"][:, 0:1], scale=1.0 / D
                           ).then_inc(std_ready, 1)
            @partial(turns, act)
            def _(g):
                for k in range(UT):
                    i = g * UT + k
                    hold(act, xn_turned, i + 1)
                    act.activation(hT[:, k, :], ps[bank[k]][:, 0:P], ACT.Identity, bias=w["gcol"][:, 3:4],
                                   scale=w["gcol"][:, 2:3]).then_inc(h_ready, 1)
                for k in range(UT):
                    i = g * UT + k
                    hold(act, up_ready, i + 1)
                    if k == 0:
                        hold(act, down_ready, g * UT)
                    for c in range(MLP // P):
                        m = act.activation(ge[:, k, c, :], ps[bank2[k]][:, c * P:c * P + P], ACT.Gelu_apprx_tanh,
                                           bias=w["b1_col"][:, c:c + 1])
                    m.then_inc(gelu_ready, 1)

        @block.tensor
        def _(pe):
            @partial(turns, pe)
            def _(g):
                for k in range(UT):
                    i = g * UT + k
                    hold(pe, att_ready, i + 1, link_s)
                    hold(pe, gt_ready, 2 * g * UT + 2 * max(k - 1, 0), link_s)
                    for j in range(q):
                        m = pe.transpose(ps[bank[k]][:, j * HW:j * HW + HW], an[:, k, j, :],
                                         s["ident"][0:HW, 0:HW])
                    m.then_inc(att_turned, 1)
                for k in range(UT):
                    i = g * UT + k
                    hold(pe, gt_ready, 2 * i + 2)
                    hold(pe, y_ready, g * UT + max(k - 1, 0))
                    for h in range(H):
                        m = pe.matmul(ps[bank2[k]][:, 0:P], gT[:, k, h, :], w["pw"][:, h, :], start=(h == 0),
                                      stop=(h == H - 1))
                    m.then_inc(proj_ready, 1)
            pe.wait_ge(x_ready, NT)
            @partial(turns, pe)
            def _(g):
                for k in range(UT):
                    i = g * UT + k
                    hold(pe, xn_ready, i + 1)
                    hold(pe, h_ready, g * UT + max(k - 1, 0))
                    pe.transpose(ps[bank[k]][:, 0:P], xn[:, k, :], s["ident"][:, :]).then_inc(xn_turned, 1)
                for k in range(UT + 1):
                    if k < UT:
                        i = g * UT + k
                        hold(pe, h_ready, i + 1)
                        hold(pe, gelu_ready, g * UT + max(k - 1, 0))
                        for c in range(MLP // P):
                            m = pe.matmul(ps[bank2[k]][:, c * P:c * P + P], w["w1"][:, c * P:c * P + P],
                                          hT[:, k, :], start=True, stop=True)
                        m.then_inc(up_ready, 1)
                    if k:
                        j = k - 1
                        i = g * UT + j
                        hold(pe, gelu_ready, i + 1)
                        hold(pe, y_ready, NT + g * UT + max(j - 1, 0))
                        for c in range(MLP // P):
                            m = pe.matmul(ps[bank3[j]][:, 0:P], ge[:, j, c, :], w["w2"][:, c, :], start=(c == 0),
                                          stop=(c == MLP // P - 1))
                        m.then_inc(down_ready, 1)


def finish(nc, sb, sem, ps, s, x, out):
    chain = sem("chain")
    x_in = sem("x_in")
    centered = sem("centered")
    squared = sem("squared")
    var_ready = sem("var_ready")
    std_ready = sem("std_ready")
    y_ready = sem("y_ready")
    stored = sem("stored")
    x0 = sb("x0", [P, NT, P], F32)
    sq = sb("sq", [P, NT, P], F32)
    var = sb("var", [P, NT], F32)
    xc = sb("xc", [P, NT, P], F32)
    xs, mean, rstd = s["xs"], s["mean"], s["rstd"]
    F = N // P
    with nc.Block() as block:
        @block.sync
        def _(sp):
            sp.dma_start(x0[:, 0:F, :], x[0:F * P, :].rearrange("(t p) d -> p t d", p=P)).then_inc(x_in, 16)
            sp.dma_start(x0[0:N - F * P, F, :], x[F * P:N, :]).then_inc(x_in, 16)
            sp.wait_ge(y_ready, 1)
            sp.dma_start(out[0:F * P, :].rearrange("(t p) d -> p t d", p=P), sq[:, 0:F, :]).then_inc(stored, 16)
            sp.dma_start(out[F * P:N, :], sq[0:N - F * P, F, :]).then_inc(stored, 16)
            sp.wait_ge(stored, 32)

        @block.vector
        def _(v):
            n = [0]

            def link(ins):
                n[0] += 1
                ins.then_inc(chain, 1)
                v.wait_ge(chain, n[0])

            v.wait_ge(x_in, 32)
            link(v.tensor_tensor(xs[:, 0:F, :], xs[:, 0:F, :], x0[:, 0:F, :], ALU.add))
            link(v.tensor_tensor(xs[0:N - F * P, F, :], xs[0:N - F * P, F, :], x0[0:N - F * P, F, :], ALU.add))
            center(v, link, xs, xc, sq, mean)
            v.tensor_copy(mean[:, 0:1], mean[:, 0:1]).then_inc(centered, 1)
            v.wait_ge(squared, 1)
            v.tensor_reduce(var[:, :], sq[:, :, :], AX, ALU.add).then_inc(var_ready, 1)
            v.wait_ge(std_ready, 1)
            link(v.reciprocal(rstd[:, :], rstd[:, :]))
            v.tensor_tensor(sq[:, :, :], xc[:, :, :], row_bc(rstd[:, :], D), ALU.mult).then_inc(y_ready, 1)

        @block.scalar
        def _(act):
            act.wait_ge(centered, 1)
            act.activation(sq[:, :, :], xc[:, :, :], ACT.Square).then_inc(squared, 1)
            act.wait_ge(var_ready, 1)
            act.activation(rstd[:, :], var[:, :], ACT.Sqrt, bias=s["eps_t"][:, 0:1], scale=1.0 / D
                           ).then_inc(std_ready, 1)


_INS = ['x', 'src', 'dst', 'L0_gnn_ln1_g', 'L0_gnn_ln1_b', 'L0_gnn_Wl', 'L0_gnn_bl', 'L0_gnn_Wr', 'L0_gnn_br',
        'L0_gnn_att', 'L0_gnn_gat_b', 'L0_gnn_proj_W', 'L0_gnn_proj_b', 'L0_gnn_ln2_g', 'L0_gnn_ln2_b', 'L0_gnn_W1',
        'L0_gnn_b1', 'L0_gnn_W2', 'L0_gnn_b2']
_OUTS = [((N, D), 'float32')]


def kernel(**inputs):
    import numpy as _np
    import concourse.bacc as _bacc
    from concourse import mybir as _mybir
    from concourse.bass_utils import run_bass_kernel_spmd as _run

    nc = _bacc.Bacc("TRN2", target_bir_lowering=False, num_devices=1)
    arrays, args = {}, []
    for name in _INS:
        a = _np.ascontiguousarray(inputs[name])
        arrays[f"in_{name}_dram"] = a
        args.append(nc.dram_tensor(f"in_{name}_dram", a.shape, _mybir.dt.from_np(a.dtype), kind="ExternalInput").ap())
    for i, (shape, dtype) in enumerate(_OUTS):
        dt = _mybir.dt.from_np(_np.dtype(dtype))
        args.append(nc.dram_tensor(f"out_{i}_dram", shape, dt, kind="ExternalOutput").ap())
    gnn(nc, *args)
    r = _run(nc, [arrays], core_ids=[0])
    got = tuple(r.results[0][f"out_{i}_dram"] for i in range(len(_OUTS)))
    return got[0]
```
